# Optimizing a Trainium2 kernel written in Bass

```python
import numpy as np
import jax
import jax.numpy as jnp

def _softmax(x, axis=-1):
    return jax.nn.softmax(x, axis=axis)

def _gelu(x):
    return jax.nn.gelu(x, approximate=True)

def _silu(x):
    return jax.nn.silu(x)

def _sigmoid(x):
    return jax.nn.sigmoid(x)

def _layernorm(x, axis=-1, eps=1e-05):
    m = jnp.mean(x, axis=axis, keepdims=True)
    v = jnp.var(x, axis=axis, keepdims=True)
    return (x - m) / jnp.sqrt(v + eps)

def _scatter_add(tgt, idx, src, axis=0):
    return tgt.at[idx].add(src)

def _segment_sum(src, seg, n):
    return jax.ops.segment_sum(src, seg, n)
kernel_name = 'mk_vit_tower_d1_tok_img512_r4_83a207'

def setup_inputs(seed: int=0):
    np.random.seed(seed)
    _w = jnp.asarray

    def _rec_inputs():
        import jax
        import jax.numpy as jnp
        _rk = jax.random.key(seed)
        x = -0.000356955 + 1 * jax.random.normal(jax.random.fold_in(_rk, 1), (64, 3, 112, 112), jnp.float32)
        return x
    x = _rec_inputs()

    def _L0_tok_setup():
        import jax, jax.numpy as jnp
        import numpy as np
        IMG = 112
        P = 16
        C = 3
        D = 128
        DC = 8
        DS = 4
        NH = IMG // P
        NPATCH = NH * NH
        PDIM = C * P * P
        BATCH = 32
        EPS = 1e-05
        key = jax.random.key(seed)
        ks = jax.random.split(key, 10)

        def lin(k, fan_in, shape):
            bound = 1.0 / np.sqrt(fan_in)
            return jax.random.uniform(k, shape, jnp.float32, -bound, bound)
        return {'images': jax.random.normal(ks[0], (BATCH, C, IMG, IMG), jnp.float32), 'W_patch': lin(ks[1], PDIM, (PDIM, D)), 'b_patch': jnp.zeros((D,), jnp.float32), 'pos_embed': jax.random.normal(ks[2], (1, NPATCH, D), jnp.float32) * 0.02, 'W_coord': lin(ks[3], D, (D, DC)), 'b_coord': jnp.zeros((DC,), jnp.float32), 'W_spinor': lin(ks[4], D, (D, DS)), 'b_spinor': jnp.zeros((DS,), jnp.float32), 'W_embed': lin(ks[5], DC, (DC, D)), 'b_embed': jnp.zeros((D,), jnp.float32), 'ln_gamma': jnp.ones((D,), jnp.float32), 'ln_beta': jnp.zeros((D,), jnp.float32), 'W_out': lin(ks[6], D, (D, D)), 'b_out': jnp.zeros((D,), jnp.float32)}
    _L0_tok_all = _L0_tok_setup()
    _L0_tok_in = {k: v for k, v in _L0_tok_all.items() if k in ('W_patch', 'b_patch', 'pos_embed', 'W_coord', 'b_coord', 'W_spinor', 'b_spinor', 'W_embed', 'b_embed', 'ln_gamma', 'ln_beta', 'W_out', 'b_out')}
    del _L0_tok_all

    def _L0_attn_setup():
        import math
        import jax, jax.numpy as jnp
        import numpy as np
        H, N, L_MAX = (128, 64, 512)
        BATCH = 8

        def _s4_forward(u, Lambda_re, Lambda_im, P, B, C, D, log_step):
            L = u.shape[1]
            Lam = jnp.minimum(Lambda_re, -0.0001) + 1j * Lambda_im
            Pc = P[..., 0] + 1j * P[..., 1]
            Bc = B[..., 0] + 1j * B[..., 1]
            Cc = C[..., 0] + 1j * C[..., 1]
            step = jnp.exp(log_step)[:, None]
            Omega = jnp.exp(jnp.arange(L) * (-2j * jnp.pi / L)).astype(jnp.complex64)
            g = 2.0 / step * ((1.0 - Omega) / (1.0 + Omega))
            c_scale = 2.0 / (1.0 + Omega)
            rec = 1.0 / (g[:, :, None] - Lam[:, None, :])

            def cau(v):
                return jnp.einsum('hn,hln->hl', v, rec)
            a0, a1 = (jnp.conj(Cc), jnp.conj(Pc))
            b0, b1 = (Bc, Pc)
            k00 = cau(a0 * b0)
            k01 = cau(a0 * b1)
            k10 = cau(a1 * b0)
            k11 = cau(a1 * b1)
            at_roots = c_scale[None, :] * (k00 - k01 * k10 / (1.0 + k11))
            K = jnp.fft.ifft(at_roots, n=L, axis=1).real.astype(u.dtype)
            fft_size = 2 * L
            U = jnp.fft.rfft(u, n=fft_size, axis=1)
            Kf = jnp.fft.rfft(K, n=fft_size, axis=1)
            Y = jnp.fft.irfft(U * Kf.T[None, :, :], n=fft_size, axis=1)[:, :L, :]
            return Y.astype(u.dtype) + u * D[None, None, :]
        key = jax.random.key(seed)
        ks = jax.random.split(key, 8)
        u = jax.random.normal(ks[0], (BATCH, L_MAX, H), dtype=jnp.float32)
        Lambda_re = -(jax.random.uniform(ks[1], (H, N), dtype=jnp.float32) * 0.5 + 0.05)
        Lambda_im = jax.random.normal(ks[2], (H, N), dtype=jnp.float32) * 3.0
        P = jax.random.normal(ks[3], (H, N, 2), dtype=jnp.float32)
        B = jax.random.normal(ks[4], (H, N, 2), dtype=jnp.float32)
        C = jax.random.normal(ks[5], (H, N, 2), dtype=jnp.float32) * 0.5 ** 0.5
        D = jnp.ones((H,), dtype=jnp.float32)
        log_step = jax.random.uniform(ks[6], (H,), dtype=jnp.float32) * (math.log(0.1) - math.log(0.001)) + math.log(0.001)
        return {'u': u, 'Lambda_re': Lambda_re, 'Lambda_im': Lambda_im, 'P': P, 'B': B, 'C': C, 'D': D, 'log_step': log_step}
    _L0_attn_all = _L0_attn_setup()
    _L0_attn_in = {k: v for k, v in _L0_attn_all.items() if k in ('Lambda_re', 'Lambda_im', 'P', 'B', 'C', 'D', 'log_step')}
    del _L0_attn_all

    def _L0_ffn_setup():
        import jax, jax.numpy as jnp
        import numpy as np
        B, S, D, F, E, NS, K = (2, 512, 128, 512, 8, 2, 2)
        key = jax.random.key(seed)
        ks = jax.random.split(key, 6)
        scale = 0.02

        def p(k, shape):
            return jax.random.normal(k, shape, jnp.float32) * scale
        return {'x': jax.random.normal(ks[0], (B, S, D), jnp.float32), 'gate_w': p(ks[1], (E, D)), 'gate_b': jnp.zeros((E,), jnp.float32), 'sw1': p(ks[2], (NS, F, D)), 'sb1': jnp.zeros((NS, F), jnp.float32), 'sw2': p(ks[3], (NS, D, F)), 'sb2': jnp.zeros((NS, D), jnp.float32), 'rw1': p(ks[4], (E, F, D)), 'rb1': jnp.zeros((E, F), jnp.float32), 'rw2': p(ks[5], (E, D, F)), 'rb2': jnp.zeros((E, D), jnp.float32)}
    _L0_ffn_all = _L0_ffn_setup()
    _L0_ffn_in = {k: v for k, v in _L0_ffn_all.items() if k in ('gate_w', 'gate_b', 'sw1', 'sb1', 'sw2', 'sb2', 'rw1', 'rb1', 'rw2', 'rb2')}
    del _L0_ffn_all
    return {'x': x, 'L0_tok_W_patch': _L0_tok_in['W_patch'], 'L0_tok_b_patch': _L0_tok_in['b_patch'], 'L0_tok_pos_embed': _L0_tok_in['pos_embed'], 'L0_tok_W_coord': _L0_tok_in['W_coord'], 'L0_tok_b_coord': _L0_tok_in['b_coord'], 'L0_tok_W_spinor': _L0_tok_in['W_spinor'], 'L0_tok_b_spinor': _L0_tok_in['b_spinor'], 'L0_tok_W_embed': _L0_tok_in['W_embed'], 'L0_tok_b_embed': _L0_tok_in['b_embed'], 'L0_tok_ln_gamma': _L0_tok_in['ln_gamma'], 'L0_tok_ln_beta': _L0_tok_in['ln_beta'], 'L0_tok_W_out': _L0_tok_in['W_out'], 'L0_tok_b_out': _L0_tok_in['b_out'], 'L0_attn_Lambda_re': _L0_attn_in['Lambda_re'], 'L0_attn_Lambda_im': _L0_attn_in['Lambda_im'], 'L0_attn_P': _L0_attn_in['P'], 'L0_attn_B': _L0_attn_in['B'], 'L0_attn_C': _L0_attn_in['C'], 'L0_attn_D': _L0_attn_in['D'], 'L0_attn_log_step': _L0_attn_in['log_step'], 'L0_ffn_gate_w': _L0_ffn_in['gate_w'], 'L0_ffn_gate_b': _L0_ffn_in['gate_b'], 'L0_ffn_sw1': _L0_ffn_in['sw1'], 'L0_ffn_sb1': _L0_ffn_in['sb1'], 'L0_ffn_sw2': _L0_ffn_in['sw2'], 'L0_ffn_sb2': _L0_ffn_in['sb2'], 'L0_ffn_rw1': _L0_ffn_in['rw1'], 'L0_ffn_rb1': _L0_ffn_in['rb1'], 'L0_ffn_rw2': _L0_ffn_in['rw2'], 'L0_ffn_rb2': _L0_ffn_in['rb2']}

def reference(x, L0_tok_W_patch, L0_tok_b_patch, L0_tok_pos_embed, L0_tok_W_coord, L0_tok_b_coord, L0_tok_W_spinor, L0_tok_b_spinor, L0_tok_W_embed, L0_tok_b_embed, L0_tok_ln_gamma, L0_tok_ln_beta, L0_tok_W_out, L0_tok_b_out, L0_attn_Lambda_re, L0_attn_Lambda_im, L0_attn_P, L0_attn_B, L0_attn_C, L0_attn_D, L0_attn_log_step, L0_ffn_gate_w, L0_ffn_gate_b, L0_ffn_sw1, L0_ffn_sb1, L0_ffn_sw2, L0_ffn_sb2, L0_ffn_rw1, L0_ffn_rb1, L0_ffn_rw2, L0_ffn_rb2):
    import jax
    import jax.numpy as jnp

    def _L0_tok_ref(images, W_patch, b_patch, pos_embed, W_coord, b_coord, W_spinor, b_spinor, W_embed, b_embed, ln_gamma, ln_beta, W_out, b_out):
        import jax, jax.numpy as jnp
        import numpy as np
        IMG = 112
        P = 16
        C = 3
        D = 128
        DC = 8
        DS = 4
        NH = IMG // P
        NPATCH = NH * NH
        PDIM = C * P * P
        BATCH = 32
        EPS = 1e-05
        B = images.shape[0]
        patches = images.reshape(B, C, NH, P, NH, P)
        patches = patches.transpose(0, 2, 4, 1, 3, 5).reshape(B, NPATCH, PDIM)
        x = patches @ W_patch + b_patch + pos_embed
        coords = x @ W_coord + b_coord
        spinor = x @ W_spinor + b_spinor
        K0 = jnp.sum(spinor * spinor, axis=-1)
        x_manifold = coords @ W_embed + b_embed
        x_enh = x_manifold * K0[..., None] + x
        mu = jnp.mean(x_enh, axis=-1, keepdims=True)
        var = jnp.mean(jnp.square(x_enh - mu), axis=-1, keepdims=True)
        x_norm = (x_enh - mu) * jax.lax.rsqrt(var + EPS) * ln_gamma + ln_beta
        return x_norm @ W_out + b_out

    def _L0_attn_ref(u, Lambda_re, Lambda_im, P, B, C, D, log_step):
        import math
        import jax, jax.numpy as jnp
        import numpy as np
        H, N, L_MAX = (128, 64, 512)
        BATCH = 8

        def _s4_forward(u, Lambda_re, Lambda_im, P, B, C, D, log_step):
            L = u.shape[1]
            Lam = jnp.minimum(Lambda_re, -0.0001) + 1j * Lambda_im
            Pc = P[..., 0] + 1j * P[..., 1]
            Bc = B[..., 0] + 1j * B[..., 1]
            Cc = C[..., 0] + 1j * C[..., 1]
            step = jnp.exp(log_step)[:, None]
            Omega = jnp.exp(jnp.arange(L) * (-2j * jnp.pi / L)).astype(jnp.complex64)
            g = 2.0 / step * ((1.0 - Omega) / (1.0 + Omega))
            c_scale = 2.0 / (1.0 + Omega)
            rec = 1.0 / (g[:, :, None] - Lam[:, None, :])

            def cau(v):
                return jnp.einsum('hn,hln->hl', v, rec)
            a0, a1 = (jnp.conj(Cc), jnp.conj(Pc))
            b0, b1 = (Bc, Pc)
            k00 = cau(a0 * b0)
            k01 = cau(a0 * b1)
            k10 = cau(a1 * b0)
            k11 = cau(a1 * b1)
            at_roots = c_scale[None, :] * (k00 - k01 * k10 / (1.0 + k11))
            K = jnp.fft.ifft(at_roots, n=L, axis=1).real.astype(u.dtype)
            fft_size = 2 * L
            U = jnp.fft.rfft(u, n=fft_size, axis=1)
            Kf = jnp.fft.rfft(K, n=fft_size, axis=1)
            Y = jnp.fft.irfft(U * Kf.T[None, :, :], n=fft_size, axis=1)[:, :L, :]
            return Y.astype(u.dtype) + u * D[None, None, :]
        return _s4_forward(u, Lambda_re, Lambda_im, P, B, C, D, log_step)

    def _L0_ffn_ref(x, gate_w, gate_b, sw1, sb1, sw2, sb2, rw1, rb1, rw2, rb2):
        import jax, jax.numpy as jnp
        import numpy as np
        B, S, D, F, E, NS, K = (2, 512, 128, 512, 8, 2, 2)
        b, s, d = x.shape
        t = x.reshape(-1, d)
        T = t.shape[0]
        hs = jax.nn.gelu(jnp.einsum('td,nfd->ntf', t, sw1) + sb1[:, None, :], approximate=False)
        shared = jnp.einsum('ntf,ndf->td', hs, sw2) + sb2.sum(axis=0)
        logits = t @ gate_w.T + gate_b
        probs = jax.nn.softmax(logits, axis=-1)
        top_v, top_i = jax.lax.top_k(probs, K)
        cw = jnp.zeros_like(probs).at[jnp.arange(T)[:, None], top_i].add(top_v)
        hr = jax.nn.gelu(jnp.einsum('td,efd->etf', t, rw1) + rb1[:, None, :], approximate=False)
        oe = jnp.einsum('etf,edf->etd', hr, rw2) + rb2[:, None, :]
        routed = jnp.einsum('etd,te->td', oe, cw)
        return (shared + routed).reshape(b, s, d)
    h = _L0_tok_ref(x, L0_tok_W_patch, L0_tok_b_patch, L0_tok_pos_embed, L0_tok_W_coord, L0_tok_b_coord, L0_tok_W_spinor, L0_tok_b_spinor, L0_tok_W_embed, L0_tok_b_embed, L0_tok_ln_gamma, L0_tok_ln_beta, L0_tok_W_out, L0_tok_b_out)
    h = h + _L0_attn_ref(_layernorm(h, axis=-1), L0_attn_Lambda_re, L0_attn_Lambda_im, L0_attn_P, L0_attn_B, L0_attn_C, L0_attn_D, L0_attn_log_step)
    h = h + _L0_ffn_ref(_layernorm(h, axis=-1), L0_ffn_gate_w, L0_ffn_gate_b, L0_ffn_sw1, L0_ffn_sb1, L0_ffn_sw2, L0_ffn_sb2, L0_ffn_rw1, L0_ffn_rb1, L0_ffn_rw2, L0_ffn_rb2)
    return h

_drawn_inputs = setup_inputs


def setup_inputs(seed=0):
    import zlib

    import numpy as np

    out = dict(_drawn_inputs(seed))
    spreads = {'L0_tok_b_patch': (0.0, 0.1),
     'L0_tok_b_coord': (0.0, 0.1),
     'L0_tok_b_spinor': (0.0, 0.1),
     'L0_tok_b_embed': (0.0, 0.1),
     'L0_tok_ln_gamma': (1.0, 0.2),
     'L0_tok_ln_beta': (0.0, 0.1),
     'L0_tok_b_out': (0.0, 0.1),
     'L0_attn_D': (1.0, 0.2),
     'L0_ffn_gate_b': (0.0, 0.8),
     'L0_ffn_sb1': (0.0, 0.751),
     'L0_ffn_sb2': (0.0, 0.1),
     'L0_ffn_rb1': (0.0, 0.8),
     'L0_ffn_rb2': (0.0, 0.8)}
    factors = {'L0_ffn_gate_w': 7.509, 'L0_ffn_rw1': 8.0, 'L0_ffn_rw2': 8.0, 'L0_ffn_sw1': 2.872}
    for name, (base, spread) in spreads.items():
        noise = np.random.default_rng([zlib.crc32(name.encode()), seed]).standard_normal(out[name].shape)
        drawn = base * np.exp(spread * noise) if base else spread * noise
        out[name] = jnp.asarray(drawn.astype(out[name].dtype))
    for name, factor in factors.items():
        out[name] = (out[name] * factor).astype(out[name].dtype)
    return out
```

```python
from contextlib import ExitStack

import concourse.bass as bass
from concourse import mybir

F32 = mybir.dt.float32
F32R = mybir.dt.float32r
ALU = mybir.AluOpType
ACT = mybir.ActivationFunctionType
AX = mybir.AxisListType

B, C, IMG, P = 64, 3, 112, 16
NH = IMG // P
L = NH * NH
D = 128
DC, DS = 8, 4
N = 64
F = 512
FO = F // 128
NS, E = 2, 8
NX = NS + E
T = B * L
PAIR = 2 * L
NPAIR = B // 2
GP = 4
GT = GP * PAIR
NG = T // GT
TILES = 4
TI = B // TILES
TR = TI * NH
HR = TR // 2
KT = C * 2
HP = D // 2
CH = HP // TILES
CONV_H = 16
LN_EPS = 1e-5
KIND = 8
V_BPATCH, V_GAMMA, V_BETA, V_RB2 = 0, 1, 2, 3
V_SB2 = V_RB2 + E
V_B1 = V_SB2 + NS
NV = V_B1 + NX * FO


def tower(nc, x, W_patch, b_patch, pos_embed, W_coord, b_coord, W_spinor, b_spinor, W_embed, b_embed,
          ln_gamma, ln_beta, W_out, b_out, Lambda_re, Lambda_im, P_, B_, C_, D_, log_step,
          gate_w, gate_b, sw1, sb1, sw2, sb2, rw1, rb1, rw2, rb2, c_ident, c_tan, c_dft, out):
    ctx = ExitStack()
    with ctx:
        base = (nc.sbuf_base + 31) // 32 * 32
        end = {}

        def place(name, shape, region, dt=F32):
            size = 4
            for n in shape[1:]:
                size *= n
            at = end[region]
            end[region] = (at + size + 31) // 32 * 32
            return nc.alloc_sbuf_tensor_at(name, shape, dt, offset=at)

        def region(name, start, size):
            end[name] = start
            return start + size

        def sem(name):
            return ctx.enter_context(nc.semaphore(name))

        at = base
        SA, SB_, SC, SH = 4 * F * NX * 4 + 512, PAIR * D * 4, 2 * NX * F * 4, NPAIR * D * 4
        region("w", at, SA); at = region("a", at, SA)
        region("y", at, SB_); region("cw", at + 2 * T * 4, 0); region("gt", at + 2 * T * 4, 0); at = region("b", at, SB_)
        region("st", at, SC); region("g", at, SC); at = region("c", at, SC)
        at = region("h", at, SH)
        region("o", at, SH); region("su", at, SH); at = region("u", at, SH)
        region("k", at, 0)

        Xc = [place(f"Xc{c}", [TR, P * IMG], "a") for c in range(C)]
        Xr = [place(f"Xr{c}", [TR, NH, P, P], "a") for c in range(C)]
        end["pt"] = end["a"]
        kt = place("kt", [L, 12, D], "pt")
        patchT = place("patchT", [128, KT, NH, TR], "a")
        xT = [place(f"xT{i}", [D, GT], "a") for i in range(2)]
        xtok = [place(f"xtok{i}", [PAIR, GP, D], "a") for i in range(2)]
        xe = [place(f"xe{i}", [PAIR, GP, D], "a") for i in range(2)]
        xnT = [place(f"xnT{i}", [D, GT], "a") for i in range(2)]
        vrows = place("vrows", [NV, D], "su")
        prow = place("prow", [L, D], "su")
        wcrow = place("wcrow", [D, DC], "su")
        wcT = place("wcT", [DC, D], "su")
        we = place("we", [DC, D], "su")
        bccol = place("bccol", [DC, 1], "su")
        bcrep = place("bcrep", [DC, PAIR], "su")
        gwrow = place("gwrow", [E, D], "su")
        lre = place("lre", [HP, 128], "su")
        lim = place("lim", [HP, 128], "su")
        praw = place("praw", [HP, 128, 2], "su")
        braw = place("braw", [HP, 128, 2], "su")
        craw = place("craw", [HP, 128, 2], "su")
        lsraw = place("lsraw", [HP, 2], "su")
        lsrep = place("lsrep", [HP, 2, N], "su")
        kk = place("kk", [L, D, KIND], "a")
        zeros = place("zeros", [L - 1, D], "su")
        hdt = place("hdt", [PAIR, GP, D], "a")
        assert end["a"] <= end["w"] + SA, (end["a"] - end["w"], SA)
        w1h = place("w1h", [D, NX, F], "w", F32R)
        w1l = place("w1l", [D, NX, F], "w", F32R)
        w2h = place("w2h", [128, NX, FO, D], "w", F32R)
        w2l = place("w2l", [128, NX, FO, D], "w", F32R)
        Tt = place("Tt", [PAIR, PAIR, D], "b")
        yh = place("yh", [D, T], "y", F32R)
        yl = place("yl", [D, T], "y", F32R)
        cwb = place("cwb", [128, E, GT], "cw")
        yt = [place(f"yt{i}", [PAIR, GP, D], "gt") for i in range(2)]
        lg = place("lg", [PAIR, NPAIR, E], "gt")
        pr = place("pr", [PAIR, NPAIR, E], "gt")
        eq = place("eq", [PAIR, NPAIR, E], "gt")
        rank = place("rank", [PAIR, NPAIR, E], "gt")
        hot = [place(f"hot{i}", [PAIR, NPAIR, E], "gt") for i in range(2)]
        cw = place("cw", [PAIR, NPAIR, E], "gt")
        red = place("red", [PAIR, NPAIR], "gt")
        cwT = place("cwT", [128, 2, PAIR], "gt")
        Wp = place("Wp", [128, KT, D], "c")
        VR = place("VR", [128, HP, 2 * KIND], "c")
        VQ = place("VQ", [128, HP, 2 * KIND], "c")
        bT = place("bT", [128, CH, L], "c")
        dT = place("dT", [128, CH, L], "c")
        RT = place("RT", [128, CH, L], "c")
        QT = place("QT", [128, CH, L], "c")
        Vr = place("Vr", [128, HP, KIND], "c")
        Vq = place("Vq", [128, HP, KIND], "c")
        prod = place("prod", [128, 14, HP], "c")
        par = place("par", [128, 8, HP], "c")
        assert end["c"] <= end["st"] + SC, end
        raw1 = place("raw1", [128, NX * FO, D], "st")
        raw2 = place("raw2", [D, NX, F], "st")
        gf = [place(f"gf{i}", [128, FO, GT], "g") for i in range(2)]
        gh = [place(f"gh{i}", [128, FO, GT], "g", F32R) for i in range(2)]
        gl = [place(f"gl{i}", [128, FO, GT], "g", F32R) for i in range(2)]
        h = place("h", [PAIR, NPAIR, D], "h")
        u = place("u", [PAIR, NPAIR, D], "u")
        acc = place("acc", [D, GT], "o")
        tmp = [place(f"tmp{i}", [D, GT], "o") for i in range(2)]
        osb = place("osb", [PAIR, GP, D], "o")
        ident = place("ident", [128, 128], "k")
        wce = place("wce", [D, D], "k")
        wsp = place("wsp", [D, DS], "k")
        wout = place("wout", [D, D], "k")
        beff = place("beff", [PAIR, D], "k")
        bout = place("bout", [PAIR, D], "k")
        dbc = place("dbc", [PAIR, D], "k")
        bsp = place("bsp", [PAIR, DS], "k")
        gbb = place("gbb", [PAIR, E], "k")
        gwT = place("gwT", [D, E], "k")
        gwh = place("gwh", [D, E], "k", F32R)
        gwl = place("gwl", [D, E], "k", F32R)
        vcol = place("vcol", [D, NV], "k")
        posb = place("posb", [D, L], "k")
        sb2s = place("sb2s", [D, 1], "k")
        tan2 = place("tan2", [128, L], "k")
        tcol = place("tcol", [L, 1], "k")
        dft = place("dft", [L, 2 * L], "k")
        s2 = place("s2", [128, HP], "k")
        a1 = place("a1", [128, HP], "k")
        a2 = place("a2", [128, HP], "k")
        eps = place("eps", [PAIR, GP], "k")
        mhalf = place("mhalf", [PAIR, GP], "k")
        mv = [place(f"mv{i}", [PAIR, GP, 2], "k") for i in range(2)]
        st = [place(f"st{i}", [PAIR, GP, 6], "k") for i in range(2)]
        rstd = [place(f"rstd{i}", [PAIR, GP], "k") for i in range(2)]
        sp = place("sp", [PAIR, 2 * GP, DS], "k")
        k0 = place("k0", [PAIR, 2 * GP], "k")
        ksb = place("ksb", [L, D], "k")
        rev = place("rev", [PAIR, E], "k")
        assert end["k"] <= nc.sbuf_usable_end, (end["k"], nc.sbuf_usable_end)
        kpad = nc.dram_tensor("kpad", [2 * L - 1, D], F32).ap()
        cwd = nc.dram_tensor("cwd", [E, T], F32).ap()
        bank = [ctx.enter_context(nc.psum_tensor(f"bank{i}", [128, 512], F32)) for i in range(8)]

        ld_par, ld_tok, ld_vec = sem("ld_par"), sem("ld_tok"), sem("ld_vec")
        ld_x = [sem(f"ld_x{c}") for c in range(C)]
        ld_raw, ld_toep = sem("ld_raw"), sem("ld_toep")
        ld_cw = [sem(f"ld_cw{e}") for e in range(E)]
        st_zero, st_k, st_cw, st_out = sem("st_zero"), sem("st_k"), sem("st_cw"), sem("st_out")
        lsrep_ready, par_T, ls_T, vec_T = sem("lsrep_ready"), sem("par_T"), sem("ls_T"), sem("vec_T")
        wcT_ready, wce_T, tok_const, s2_ready = sem("wcT_ready"), sem("wce_T"), sem("tok_const"), sem("s2_ready")
        zero_ready, v_zeroed, pool_const, toep_zeroed = sem("zero_ready"), sem("v_zeroed"), sem("pool_const"), sem("toep_zeroed")
        b_ready, sq_ready, rec_ready, r_ready, q_ready = (sem(n) for n in ("b_ready", "sq_ready", "rec_ready", "r_ready", "q_ready"))
        cauchy_done, kk_ready, at_ready, k_T, k_ready = (sem(n) for n in ("cauchy_done", "kk_ready", "at_ready", "k_T", "k_ready"))
        tp_done = [sem(f"tp_done{i}") for i in range(2)]
        tp_copied = [sem(f"tp_copied{i}") for i in range(2)]
        x_sorted = [sem(f"x_sorted{c}") for c in range(C)]
        proj_done, xT_ready, a_done, mani_read, xtok_ready, xtok_used, stats_ready, rstd_ready, xn_ready = (
            [sem(f"{n}{i}") for i in range(2)] for n in
            ("proj_done", "xT_ready", "a_done", "mani_read", "xtok_ready", "xtok_used", "stats_ready", "rstd_ready", "xn_ready"))
        xnT_done, xnT_ready, wout_done, h_ready, u_ready, hd_ready = (
            [sem(f"{n}{i}") for i in range(2)] for n in
            ("xnT_done", "xnT_ready", "wout_done", "h_ready", "u_ready", "hd_ready"))
        w_T, w_hi, w_lo = sem("w_T"), sem("w_hi"), sem("w_lo")
        conv_done, conv_read = sem("conv_done"), sem("conv_read")
        stats2, rstd2, y_ready, y_T, yh_ready, yl_ready = (sem(n) for n in ("stats2", "rstd2", "y_ready", "y_T", "yh_ready", "yl_ready"))
        gate_done, lg_ready, exp_ready, cw_ready, cw_T, cwT_ready = (sem(n) for n in ("gate_done", "lg_ready", "exp_ready", "cw_ready", "cw_T", "cwT_ready"))
        up_done, act_done, split_done, down_done = sem("up_done"), sem("act_done"), sem("split_done"), sem("down_done")
        scaled, added, out_T, out_ready = sem("scaled"), sem("added"), sem("out_T"), sem("out_ready")

        block = ctx.enter_context(nc.Block())

        def pairs(k, half):
            return bass.ds(2 * GP * k + GP * half, GP)

        @block.sync
        def _(sp_):
            def load_x(k, c):
                src = x[bass.ds(TI * k, TI), c].rearrange("b (p i) w -> b p (i w)", p=NH)
                sp_.dma_start(Xc[c][:, :], src).then_inc(ld_x[c], 16)

            for c in range(C):
                load_x(0, c)
            sp_.wait_ge(zero_ready, 1)
            sp_.dma_start(kpad[L:2 * L - 1, :], zeros[:, :]).then_inc(st_zero, 16)
            with sp_.Fori(1, TILES) as k:
                for c in range(C):
                    sp_.wait_ge(x_sorted[c], k)
                    load_x(k, c)
            sp_.wait_ge(cauchy_done, TILES)
            for dst, src in ((raw1[:, 0:NS * FO, :], sw1), (raw1[:, NS * FO:NX * FO, :], rw1)):
                sp_.dma_start(dst, src.rearrange("e (o p) d -> p (e o) d", p=128)).then_inc(ld_raw, 16)
            for dst, src in ((raw2[:, 0:NS, :], sw2), (raw2[:, NS:NX, :], rw2)):
                sp_.dma_start(dst, src.rearrange("e d f -> d e f")).then_inc(ld_raw, 16)
            sp_.wait_ge(k_ready, 1)
            sp_.dma_start(kpad[0:L, :], ksb[:, :]).then_inc(st_k, 16)
            sp_.wait_ge(st_k, 16)
            sp_.wait_ge(st_zero, 16)
            sp_.wait_ge(toep_zeroed, 1)
            for b in range(2):
                src = bass.AP(kpad.tensor, (L - 1) * D, [[D, L], [-D, L], [1, D]])
                sp_.dma_start(Tt[b * L:(b + 1) * L, b * L:(b + 1) * L, :], src).then_inc(ld_toep, 16)
            sp_.wait_ge(cwT_ready, 1)
            for blk in range(2):
                for q in range(16):
                    dst = cwd[:, (blk * 16 + q) * PAIR:(blk * 16 + q + 1) * PAIR]
                    sp_.dma_start(dst, cwT[q * E:(q + 1) * E, blk, :]).then_inc(st_cw, 16)
            sp_.wait_ge(st_cw, 32 * 16)

            def load_cw(c, e):
                src = cwd[e:e + 1, bass.ds(GT * c, GT)].broadcast_to([128, GT])
                sp_.dma_start(cwb[:, e, :], src).then_inc(ld_cw[e], 16)

            def store(c):
                sp_.wait_ge(out_ready, c + 1)
                dst = out.rearrange("b l d -> (b l) d")[bass.ds(GT * c, GT), :].rearrange("(p i) d -> i p d", p=GP)
                sp_.dma_start(dst, osb[:, :, :]).then_inc(st_out, 16)

            for e in range(E):
                load_cw(0, e)
            with sp_.Fori(1, NG) as c:
                for e in range(E):
                    if e == 4:
                        store(c - 1)
                    sp_.wait_ge(scaled, 9 * (c - 1) + e + 2)
                    load_cw(c, e)
            store(NG - 1)
            sp_.wait_ge(st_out, 16 * NG)

        @block.gpsimd
        def _(pool):
            nc.gpsimd.memset(VR[:, :, :], 0.0)
            nc.gpsimd.memset(VQ[:, :, :], 0.0).then_inc(v_zeroed, 1)
            nc.gpsimd.memset(zeros[:, :], 0.0).then_inc(zero_ready, 1)
            for e in range(E):
                nc.gpsimd.memset(rev[:, e:e + 1], float(E - e))
            nc.gpsimd.memset(eps[:, :], LN_EPS)
            nc.gpsimd.memset(mhalf[:, :], -0.5).then_inc(pool_const, 1)

            def sort_pixels(k, first):
                for c in range(C):
                    pool.wait_ge(ld_x[c], 16 * (k + 1))
                    if not first:
                        pool.wait_ge(tp_done[1], KT * (k - 1) + 2 * c + 2)
                    nc.gpsimd.tensor_copy(Xr[c][:, :, :, :].rearrange("r w i j -> r i w j"),
                                          Xc[c][:, :].rearrange("r (i w j) -> r i w j", i=P, w=NH)).then_inc(x_sorted[c], 1)

            sort_pixels(0, True)
            nc.gpsimd.memset(Tt[:, :, :], 0.0).then_inc(toep_zeroed, 1)

            def inv_std(half, done):
                nc.gpsimd.tensor_tensor(rstd[half][:, :], mv[half][:, :, 1], eps[:, :], ALU.add)
                pool.drain()
                nc.gpsimd.tensor_tensor(rstd[half][:, :], rstd[half][:, :], mhalf[:, :], ALU.pow).then_inc(done, 1)

            def tile(k, more):
                if more:
                    sort_pixels(k + 1, False)
                pool.wait_ge(rec_ready, k + 1)
                pool.wait_ge(cauchy_done, k)
                nc.gpsimd.tensor_tensor(QT[:, :, :], dT[:, :, :], bT[:, :, :], ALU.mult).then_inc(q_ready, 1)
                for n in range(2):
                    for half in range(2):
                        pool.wait_ge(stats_ready[half], 2 * k + n + 1)
                        inv_std(half, rstd_ready[half])
                for half in range(2):
                    pool.wait_ge(u_ready[half], k + 1)
                    nc.gpsimd.tensor_tensor(hdt[:, :, :], u[:, pairs(k, half), :],
                                            dbc[:, :].unsqueeze(1).broadcast_to([PAIR, GP, D]), ALU.mult)
                    pool.drain()
                    nc.gpsimd.tensor_tensor(h[:, pairs(k, half), :], h[:, pairs(k, half), :], hdt[:, :, :],
                                            ALU.add).then_inc(hd_ready[half], 1)
                    pool.drain()
            for k in range(TILES):
                tile(k, k + 1 < TILES)
            for j in range(NG):
                pool.wait_ge(stats2, j + 1)
                inv_std(j % 2, rstd2)
            with pool.Fori(0, NG) as c:
                for e in range(E):
                    pool.wait_ge(scaled, 9 * c + e + 2)
                    nc.gpsimd.tensor_tensor(acc[:, :], acc[:, :], tmp[e % 2][:, :], ALU.add).then_inc(added, 1)
                    pool.drain()

        @block.scalar
        def _(act):
            def load(dst, src, s):
                act.dma_start(dst, src).then_inc(s, 16)

            load(ident[:, :], c_ident, ld_par)
            load(lsraw[:, :], log_step.rearrange("(a b) -> a b", b=2), ld_par)
            for dst, src in ((praw, P_), (braw, B_), (craw, C_)):
                load(dst[:, :, :], src.rearrange("(a b) n t -> a (b n) t", b=2), ld_par)
            for dst, src in ((lre, Lambda_re), (lim, Lambda_im)):
                load(dst[:, :], src.rearrange("(a b) n -> a (b n)", b=2), ld_par)
            load(tan2[:, :], c_tan[0:1, :].broadcast_to([128, L]), ld_par)
            load(tcol[:, :], c_tan[1, :].unsqueeze(1), ld_par)
            load(dft[:, :], c_dft, ld_par)

            def rows(v):
                return v.unsqueeze(0)

            for at, src in ((V_BPATCH, rows(b_patch)), (V_GAMMA, rows(ln_gamma)), (V_BETA, rows(ln_beta)), (V_RB2, rb2),
                            (V_SB2, sb2), (V_B1, sb1.rearrange("e (o p) -> (e o) p", p=128)),
                            (V_B1 + NS * FO, rb1.rearrange("e (o p) -> (e o) p", p=128))):
                load(vrows[at:at + src.shape[0], :], src, ld_vec)
            load(prow[:, :], pos_embed[0], ld_vec)
            load(wcrow[:, :], W_coord, ld_vec)
            load(gwrow[:, :], gate_w, ld_vec)
            load(we[:, :], W_embed, ld_vec)
            load(bccol[:, :], b_coord.unsqueeze(1), ld_vec)
            load(Wp[:, :, :], W_patch.rearrange("(t p) d -> p t d", p=128), ld_tok)
            load(wsp[:, :], W_spinor, ld_tok)
            load(wout[:, :], W_out, ld_tok)
            load(beff[:, :], rows(b_embed).broadcast_to([PAIR, D]), ld_tok)
            load(bout[:, :], rows(b_out).broadcast_to([PAIR, D]), ld_tok)
            load(dbc[:, :], rows(D_).broadcast_to([PAIR, D]), ld_tok)
            load(bsp[:, :], rows(b_spinor).broadcast_to([PAIR, DS]), ld_tok)
            load(gbb[:, :], rows(gate_b).broadcast_to([PAIR, E]), ld_tok)

            act.wait_ge(ls_T, 1)
            nc.scalar.activation(s2[:, :], bank[4][:, 0:HP], ACT.Exp, scale=-1.0).then_inc(s2_ready, 1)

            def copy_patches(k):
                for t in range(KT):
                    for i, (lo, hi) in enumerate(((0, 4), (4, NH))):
                        act.wait_ge(tp_done[i], KT * k + t + 1)
                        nc.scalar.copy(patchT[:, t, lo:hi, :].rearrange("p w r -> p (w r)"),
                                       bank[i][:, 0:(hi - lo) * TR]).then_inc(tp_copied[i], 1)

            def tile(k, more):
                act.wait_ge(b_ready, k + 1)
                nc.scalar.activation(dT[:, :, :], bT[:, :, :], ACT.Square).then_inc(sq_ready, 1)
                for half in range(2):
                    act.wait_ge(a_done[half], k + 1)
                    act.wait_ge(xtok_used[half], k)
                    nc.scalar.copy(xtok[half][:, :, :].rearrange("p g d -> p (g d)"), bank[6][0:PAIR, :]).then_inc(xtok_ready[half], 1)
                act.wait_ge(cauchy_done, k + 1)
                nc.scalar.copy(kk[:, bass.ds(2 * CH * k, 2 * CH), :].rearrange("p c v -> p (c v)"),
                               bank[3][0:L, 0:2 * CH * KIND]).then_inc(kk_ready, 1)
                if more:
                    copy_patches(k + 1)
                else:
                    act.wait_ge(k_T, 1)
                    nc.scalar.copy(ksb[:, :], bank[3][0:L, 384:512]).then_inc(k_ready, 1)
                for half in range(2):
                    act.wait_ge(xnT_done[half], k + 1)
                    act.wait_ge(wout_done[half], k)
                    nc.scalar.activation(xnT[half][:, :], bank[7][:, 0:GT], ACT.Identity, scale=vcol[:, V_GAMMA:V_GAMMA + 1],
                                         bias=vcol[:, V_BETA:V_BETA + 1]).then_inc(xnT_ready[half], 1)

            act.wait_ge(tok_const, 1)
            copy_patches(0)
            tile(0, True)
            with act.Fori(1, TILES - 1) as k:
                tile(k, True)
            tile(TILES - 1, False)

            for half in range(2):
                act.wait_ge(u_ready[half], TILES)
                act.wait_ge(hd_ready[half], TILES)
            act.wait_ge(st_zero, 16)
            for i in range(2 * NX):
                act.wait_ge(w_T, i + 1)
                hi = (w1h[:, i // 2, :], w2h[:, i // 2, :, :].rearrange("p o d -> p (o d)"))[i % 2]
                nc.scalar.copy(hi, bank[i % 3][:, :]).then_inc(w_hi, 1)
            for j in range(NG):
                act.wait_ge(y_T, j + 1)
                nc.scalar.copy(yh[:, j * GT:(j + 1) * GT], bank[4 + j % 4][:, 0:GT]).then_inc(yh_ready, 1)
            act.wait_ge(lg_ready, 1)
            nc.scalar.activation(pr[:, :, :], lg[:, :, :], ACT.Exp).then_inc(exp_ready, 1)

            def chunk(c, first):
                for e in range(NX):
                    for o in range(FO):
                        act.wait_ge(up_done, FO * NX * c + FO * e + o + 1)
                        if o == 0 and not (first and e < 2):
                            act.wait_ge(split_done, 2 * (NX * c + e - 1))
                        nc.scalar.activation(gf[e % 2][:, o, :], bank[o][:, 0:GT], ACT.Gelu,
                                             bias=vcol[:, V_B1 + FO * e + o:V_B1 + FO * e + o + 1]).then_inc(act_done, 1)

            chunk(0, True)
            with act.Fori(1, NG) as c:
                chunk(c, False)

        @block.vector
        def _(dve):
            V = nc.vector
            dve.wait_ge(ld_par, 16 * 10)
            V.tensor_copy(lsrep[:, :, :], lsraw[:, :].unsqueeze(2).broadcast_to([HP, 2, N])).then_inc(lsrep_ready, 1)
            dve.wait_ge(par_T, 1)
            V.tensor_copy(par[:, :, :].rearrange("p a b -> p (a b)"), bank[3][:, :])
            dve.drain()
            Pr, Pi, Br, Bi, Cr, Ci, Lr, Li = (par[:, i, :] for i in range(8))
            V.tensor_scalar(a1[:, :], Lr, -1.0, 1e-4, ALU.mult, ALU.max)
            products = [(Cr, Br), (Ci, Bi), (Cr, Bi), (Ci, Br), (Cr, Pr), (Ci, Pi), (Cr, Pi), (Ci, Pr),
                        (Pr, Br), (Pi, Bi), (Pr, Bi), (Pi, Br), (Pr, Pr), (Pi, Pi)]
            for i, (p, q) in enumerate(products):
                V.tensor_tensor(prod[:, i, :], p, q, ALU.mult)
            V.memset(Vr[:, :, KIND - 1], 0.0)
            dve.drain()
            V.tensor_tensor(a2[:, :], a1[:, :], a1[:, :], ALU.mult)
            for i in range(7):
                V.tensor_tensor(Vr[:, :, i], prod[:, 2 * i, :], prod[:, 2 * i + 1, :], ALU.subtract if i in (1, 3, 5) else ALU.add)
            dve.drain()
            V.tensor_copy(Vq[:, :, 0:KIND:2], Vr[:, :, 1:KIND:2])
            V.tensor_scalar(Vq[:, :, 1:KIND:2], Vr[:, :, 0:KIND:2], -1.0, None, ALU.mult)
            dve.drain()
            dve.wait_ge(v_zeroed, 1)
            for b in range(2):
                rows_ = slice(64 * b, 64 * b + 64)
                V.tensor_copy(VR[rows_, :, KIND * b:KIND * (b + 1)], Vr[rows_, :, :])
                V.tensor_copy(VQ[rows_, :, KIND * b:KIND * (b + 1)], Vq[rows_, :, :])
            dve.wait_ge(vec_T, 1)
            dve.wait_ge(ld_vec, 16 * 12)
            V.tensor_copy(vcol[:, :], bank[5][:, 0:NV])
            V.tensor_copy(wcT[:, :], bank[5][0:DC, 128:256])
            V.tensor_copy(gwT[:, :], bank[5][:, 256:256 + E])
            V.tensor_copy(gwh[:, :], bank[5][:, 256:256 + E])
            V.tensor_copy(bcrep[:, :], bccol[:, :].broadcast_to([DC, PAIR])).then_inc(wcT_ready, 1)
            dve.drain()
            V.tensor_tensor(gwl[:, :], gwT[:, :], gwh[:, :].bitcast(F32), ALU.subtract)
            V.tensor_scalar(posb[:, :], bank[5][:, 64:64 + L], vcol[:, V_BPATCH:V_BPATCH + 1], None, ALU.add)
            V.tensor_tensor(sb2s[:, :], vcol[:, V_SB2:V_SB2 + 1], vcol[:, V_SB2 + 1:V_SB2 + 2], ALU.add)
            dve.wait_ge(wce_T, 1)
            dve.wait_ge(ld_tok, 16 * 8)
            V.tensor_copy(wce[:, :], bank[6][:, 0:D])
            V.tensor_tensor(beff[:, :], beff[:, :], bank[6][0:PAIR, D:2 * D], ALU.add).then_inc(tok_const, 1)
            dve.wait_ge(s2_ready, 1)
            dve.wait_ge(pool_const, 1)
            dve.drain()

            def over_l(v, k):
                return v[:, bass.ds(CH * k, CH)].unsqueeze(2).broadcast_to([128, CH, L])

            def cauchy_b(k):
                dve.wait_ge(q_ready, k)
                V.tensor_tensor(bT[:, :, :], over_l(s2, k), tan2[:, :].unsqueeze(1).broadcast_to([128, CH, L]), ALU.mult)
                dve.drain()
                V.tensor_tensor(bT[:, :, :], bT[:, :, :], over_l(par[:, 7, :], k), ALU.subtract).then_inc(b_ready, 1)

            def cauchy_r(k):
                dve.wait_ge(sq_ready, k + 1)
                V.tensor_tensor(dT[:, :, :], dT[:, :, :], over_l(a2, k), ALU.add)
                dve.drain()
                V.reciprocal(dT[:, :, :], dT[:, :, :]).then_inc(rec_ready, 1)
                dve.drain()
                dve.wait_ge(cauchy_done, k)
                V.tensor_tensor(RT[:, :, :], dT[:, :, :], over_l(a1, k), ALU.mult).then_inc(r_ready, 1)

            def token_stats(half, src):
                for g in range(GP):
                    V.bn_stats(st[half][:, g, :], src[:, g, :])
                dve.drain()
                for g in range(GP):
                    last = V.bn_aggr(mv[half][:, g, :], st[half][:, g, :])
                return last

            def normalize(half, dst, src):
                for g in range(GP):
                    last = V.tensor_scalar(dst[:, g, :], src[:, g, :], mv[half][:, g, 0:1], rstd[half][:, g:g + 1],
                                           ALU.subtract, ALU.mult)
                return last

            def evacuate_x(k, half):
                dve.wait_ge(proj_done[half], k + 1)
                dve.wait_ge(a_done[half], k)
                V.tensor_tensor(xT[half][:, :].rearrange("p (b h w) -> p b h w", b=HR // NH, h=NH),
                                bank[2][:, 0:GT].rearrange("p (w b h) -> p b h w", w=NH, h=NH),
                                posb[:, :].rearrange("p (h w) -> p h w", h=NH).unsqueeze(1).broadcast_to([D, HR // NH, NH, NH]),
                                ALU.add).then_inc(xT_ready[half], 1)

            def spinors(k):
                dve.wait_ge(a_done[1], k + 1)
                V.tensor_tensor(sp[:, :, :], bank[7][0:PAIR, GT:GT + 2 * GP * DS].rearrange("p (g s) -> p g s", s=DS),
                                bsp[:, :].unsqueeze(1).broadcast_to([PAIR, 2 * GP, DS]), ALU.add)
                dve.drain()
                V.tensor_tensor(sp[:, :, :], sp[:, :, :], sp[:, :, :], ALU.mult)
                dve.drain()
                V.tensor_reduce(k0[:, :], sp[:, :, :], AX.X, ALU.add)

            def enhance(k, half):
                V.tensor_tensor(xe[half][:, :, :], bank[4 + half][0:PAIR, :].rearrange("p (g d) -> p g d", g=GP),
                                beff[:, :].unsqueeze(1).broadcast_to([PAIR, GP, D]), ALU.add).then_inc(mani_read[half], 1)
                dve.drain()
                dve.wait_ge(xtok_ready[half], k + 1)
                for g in range(GP):
                    last = V.scalar_tensor_tensor(xe[half][:, g, :], xe[half][:, g, :], k0[:, GP * half + g:GP * half + g + 1], xtok[half][:, g, :],
                                                  ALU.mult, ALU.add)
                last.then_inc(xtok_used[half], 1)
                dve.drain()
                token_stats(half, xe[half][:, :, :]).then_inc(stats_ready[half], 1)

            def first_norm(k, half):
                dve.wait_ge(rstd_ready[half], 2 * k + 1)
                normalize(half, xe[half][:, :, :], xe[half][:, :, :]).then_inc(xn_ready[half], 1)

            def tokenized(k, half):
                dve.wait_ge(wout_done[half], k + 1)
                dst = h[:, pairs(k, half), :]
                V.tensor_tensor(dst, bank[4 + half][0:PAIR, :].rearrange("p (g d) -> p g d", g=GP),
                                bout[:, :].unsqueeze(1).broadcast_to([PAIR, GP, D]), ALU.add).then_inc(h_ready[half], 1)
                dve.drain()
                for g in range(GP):
                    V.bn_stats(st[half][:, g, :], h[:, 2 * GP * k + GP * half + g, :])
                dve.drain()
                for g in range(GP):
                    last = V.bn_aggr(mv[half][:, g, :], st[half][:, g, :])
                last.then_inc(stats_ready[half], 1)

            def conv_input(k, half):
                dve.wait_ge(rstd_ready[half], 2 * k + 2)
                for g in range(GP):
                    p = 2 * GP * k + GP * half + g
                    last = V.tensor_scalar(u[:, p, :], h[:, p, :], mv[half][:, g, 0:1], rstd[half][:, g:g + 1], ALU.subtract, ALU.mult)
                last.then_inc(u_ready[half], 1)

            def at_roots():
                dve.wait_ge(kk_ready, TILES)
                r00, i00, r01, i01, r10, i10, r11, i11 = (kk[:, :, i] for i in range(KIND))
                t = [kt[:, i, :] for i in range(12)]

                def tt(o, a, b, op):
                    V.tensor_tensor(t[o], a, b, op)

                tt(0, r01, r10, ALU.mult); tt(1, i01, i10, ALU.mult); tt(2, r01, i10, ALU.mult); tt(3, i01, r10, ALU.mult)
                V.tensor_scalar(t[4], r11, 1.0, None, ALU.add); tt(5, i11, i11, ALU.mult)
                dve.drain()
                tt(6, t[0], t[1], ALU.subtract); tt(7, t[2], t[3], ALU.add); tt(8, t[4], t[4], ALU.mult)
                dve.drain()
                tt(8, t[8], t[5], ALU.add); tt(0, t[6], t[4], ALU.mult); tt(1, t[7], i11, ALU.mult)
                tt(2, t[7], t[4], ALU.mult); tt(3, t[6], i11, ALU.mult)
                dve.drain()
                V.reciprocal(t[8], t[8]); tt(0, t[0], t[1], ALU.add); tt(2, t[2], t[3], ALU.subtract)
                dve.drain()
                tt(0, t[0], t[8], ALU.mult); tt(2, t[2], t[8], ALU.mult)
                dve.drain()
                tt(0, r00, t[0], ALU.subtract); tt(2, i00, t[2], ALU.subtract)
                dve.drain()
                V.tensor_scalar(t[1], t[2], tcol[:, 0:1], None, ALU.mult); V.tensor_scalar(t[3], t[0], tcol[:, 0:1], None, ALU.mult)
                dve.drain()
                tt(10, t[0], t[1], ALU.subtract)
                V.tensor_tensor(t[11], t[2], t[3], ALU.add).then_inc(at_ready, 1)

            def tile(k, more):
                cauchy_b(k)
                for half in range(2):
                    evacuate_x(k, half)
                cauchy_r(k)
                spinors(k)
                for half in range(2):
                    enhance(k, half)
                if not more:
                    at_roots()
                for half in range(2):
                    first_norm(k, half)
                for half in range(2):
                    tokenized(k, half)
                for half in range(2):
                    conv_input(k, half)
                dve.drain()

            tile(0, True)
            with dve.Fori(1, TILES - 1) as k:
                tile(k, True)
            tile(TILES - 1, False)

            for i in range(2 * NX):
                dve.wait_ge(w_hi, i + 1)
                hi = (w1h[:, i // 2, :], w2h[:, i // 2, :, :].rearrange("p o d -> p (o d)"))[i % 2]
                lo = (w1l[:, i // 2, :], w2l[:, i // 2, :, :].rearrange("p o d -> p (o d)"))[i % 2]
                V.tensor_tensor(lo, bank[i % 3][:, :], hi.bitcast(F32), ALU.subtract).then_inc(w_lo, 1)
            for half in range(2):
                dve.wait_ge(hd_ready[half], TILES)
            for i in range(D // CONV_H):
                dve.wait_ge(conv_done, i + 1)
                part = h[:, :, i * CONV_H:(i + 1) * CONV_H]
                V.tensor_tensor(part, part, bank[4 + i % 4][0:PAIR, :].rearrange("p (c g) -> p g c", c=CONV_H),
                                ALU.add).then_inc(conv_read, 1)
            dve.drain()

            def second_stats(j):
                token_stats(j % 2, h[:, j * GP:(j + 1) * GP, :]).then_inc(stats2, 1)

            def low_y(j):
                dve.wait_ge(yh_ready, j + 1)
                span = slice(j * GT, (j + 1) * GT)
                V.tensor_tensor(yl[:, span], bank[4 + j % 4][:, 0:GT], yh[:, span].bitcast(F32), ALU.subtract).then_inc(yl_ready, 1)

            second_stats(0)
            for j in range(NG):
                if j + 1 < NG:
                    second_stats(j + 1)
                dve.wait_ge(rstd2, j + 1)
                if j >= 2:
                    dve.wait_ge(y_T, j - 1)
                normalize(j % 2, yt[j % 2][:, :, :], h[:, j * GP:(j + 1) * GP, :]).then_inc(y_ready, 1)
                dve.drain()
                if j >= 1:
                    low_y(j - 1)
            low_y(NG - 1)

            def wide(v):
                return v[:, :].unsqueeze(2).broadcast_to([PAIR, NPAIR, E])

            revb = rev[:, :].unsqueeze(1).broadcast_to([PAIR, NPAIR, E])
            dve.wait_ge(gate_done, 1)
            V.tensor_tensor(lg[:, :, :], bank[3][0:PAIR, 0:NPAIR * E].rearrange("p (g e) -> p g e", e=E),
                            gbb[:, :].unsqueeze(1).broadcast_to([PAIR, NPAIR, E]), ALU.add)
            dve.drain()
            V.tensor_reduce(red[:, :], lg[:, :, :], AX.X, ALU.max)
            dve.drain()
            V.tensor_tensor(lg[:, :, :], lg[:, :, :], wide(red), ALU.subtract).then_inc(lg_ready, 1)
            dve.wait_ge(exp_ready, 1)
            V.tensor_reduce(red[:, :], pr[:, :, :], AX.X, ALU.add)
            dve.drain()
            V.reciprocal(red[:, :], red[:, :])
            dve.drain()
            V.tensor_tensor(pr[:, :, :], pr[:, :, :], wide(red), ALU.mult)
            dve.drain()
            for n, src in enumerate((pr, lg)):
                V.tensor_reduce(red[:, :], src[:, :, :], AX.X, ALU.max)
                dve.drain()
                V.tensor_tensor(eq[:, :, :], src[:, :, :], wide(red), ALU.is_equal)
                dve.drain()
                V.tensor_tensor(rank[:, :, :], eq[:, :, :], revb, ALU.mult)
                dve.drain()
                V.tensor_reduce(red[:, :], rank[:, :, :], AX.X, ALU.max)
                dve.drain()
                V.tensor_tensor(hot[n][:, :, :], rank[:, :, :], wide(red), ALU.is_equal)
                dve.drain()
                if n == 0:
                    V.scalar_tensor_tensor(lg[:, :, :], hot[0][:, :, :], -2.0, pr[:, :, :], ALU.mult, ALU.add)
                    dve.drain()
            V.tensor_tensor(eq[:, :, :], hot[0][:, :, :], hot[1][:, :, :], ALU.add)
            dve.drain()
            V.tensor_tensor(cw[:, :, :], eq[:, :, :], pr[:, :, :], ALU.mult).then_inc(cw_ready, 1)
            dve.wait_ge(cw_T, 1)
            V.tensor_copy(cwT[:, :, :].rearrange("p a b -> p (a b)"), bank[7][:, 0:2 * PAIR]).then_inc(cwT_ready, 1)

            def split(c, e, first):
                for p in range(2):
                    dve.wait_ge(act_done, FO * NX * c + FO * e + 2 * p + 2)
                    if p == 0 and not (first and e < 2):
                        dve.wait_ge(down_done, NX * c + e - 1)
                    span = slice(2 * p, 2 * p + 2)
                    V.tensor_copy(gh[e % 2][:, span, :], gf[e % 2][:, span, :])
                    dve.drain()
                    V.tensor_tensor(gl[e % 2][:, span, :], gf[e % 2][:, span, :], gh[e % 2][:, span, :].bitcast(F32),
                                    ALU.subtract).then_inc(split_done, 1)

            def combine(c, unit, first):
                src = bank[4 + unit % 3][:, 0:GT]
                dve.wait_ge(down_done, NX * c + unit + 2)
                if unit == 0:
                    if not first:
                        dve.wait_ge(out_T, c)
                    V.tensor_scalar(acc[:, :], src, sb2s[:, 0:1], None, ALU.add).then_inc(scaled, 1)
                    return
                e = unit - 1
                dve.wait_ge(ld_cw[e], 16 * (c + 1))
                if not (first and e < 2):
                    dve.wait_ge(added, E * c + e - 1)
                V.scalar_tensor_tensor(tmp[e % 2][:, :], src, vcol[:, V_RB2 + e:V_RB2 + e + 1], cwb[:, e, :],
                                       ALU.add, ALU.mult).then_inc(scaled, 1)

            def output(c, first):
                dve.wait_ge(out_T, c + 1)
                if not first:
                    dve.wait_ge(st_out, 16 * c)
                V.tensor_tensor(osb[:, :, :], bank[7][0:PAIR, :].rearrange("p (g d) -> p g d", g=GP),
                                h[:, bass.ds(GP * c, GP), :], ALU.add).then_inc(out_ready, 1)

            def chunk(c, first, second):
                for e in range(NX):
                    split(c, e, first)
                    if e == 0 and not first:
                        combine(c - 1, NX - 2, second)
                    if e == 2 and not first:
                        output(c - 1, second)
                    if e >= 2:
                        combine(c, e - 2, first)

            chunk(0, True, False)
            chunk(1, False, True)
            with dve.Fori(2, NG) as c:
                chunk(c, False, False)
            combine(NG - 1, NX - 2, False)
            output(NG - 1, False)

        @block.tensor
        def _(pe):
            MM, TP = nc.tensor.matmul, nc.tensor.transpose

            def to_columns(dst, src):
                rows_ = src.shape[0]
                return TP(dst, src, ident[0:rows_, 0:rows_])

            pe.wait_ge(ld_par, 16 * 10)
            for i, src in enumerate((praw[:, :, 0], praw[:, :, 1], braw[:, :, 0], braw[:, :, 1], craw[:, :, 0], craw[:, :, 1],
                                     lre[:, :], lim[:, :])):
                last = to_columns(bank[3][:, i * HP:(i + 1) * HP], src)
            last.then_inc(par_T, 1)
            pe.wait_ge(lsrep_ready, 1)
            to_columns(bank[4][:, 0:HP], lsrep[:, :, :].rearrange("p b n -> p (b n)")).then_inc(ls_T, 1)
            pe.wait_ge(ld_vec, 16 * 12)
            to_columns(bank[5][:, 0:NV], vrows[:, :])
            to_columns(bank[5][:, 64:64 + L], prow[:, :])
            to_columns(bank[5][0:DC, 128:256], wcrow[:, :])
            to_columns(bank[5][:, 256:256 + E], gwrow[:, :]).then_inc(vec_T, 1)
            pe.wait_ge(wcT_ready, 1)
            MM(bank[6][:, 0:D], wcT[:, :], we[:, :], start=True, stop=True)
            MM(bank[6][0:PAIR, D:2 * D], bcrep[:, :], we[:, :], start=True, stop=True).then_inc(wce_T, 1)

            def transpose_patches(k):
                for t in range(KT):
                    c, top = t // 2, t % 2
                    if top == 0:
                        pe.wait_ge(x_sorted[c], k + 1)
                    src = Xr[c][:, :, top * 8:top * 8 + 8, :].rearrange("r w i j -> r w (i j)")
                    for i, (lo, hi) in enumerate(((0, 4), (4, NH))):
                        pe.wait_ge(tp_copied[i], KT * k + t)
                        for w in range(lo, hi):
                            last = to_columns(bank[i][:, (w - lo) * TR:(w - lo + 1) * TR], src[:, w, :])
                        last.then_inc(tp_done[i], 1)

            def project(k, half):
                if half == 0:
                    for i in range(2):
                        pe.wait_ge(tp_copied[i], KT * (k + 1))
                    pe.wait_ge(xT_ready[1], k)
                else:
                    pe.wait_ge(xT_ready[0], k + 1)
                for t in range(KT):
                    last = MM(bank[2][:, 0:GT], Wp[:, t, :], patchT[:, t, :, half * HR:(half + 1) * HR],
                              start=t == 0, stop=t == KT - 1)
                last.then_inc(proj_done[half], 1)

            def embed(k, half):
                pe.wait_ge(xT_ready[half], k + 1)
                pe.wait_ge(h_ready[half], k)
                if half == 0:
                    pe.wait_ge(xtok_ready[1], k)
                    pe.wait_ge(xnT_ready[1], k)
                else:
                    pe.wait_ge(xtok_ready[0], k + 1)
                for g in range(GP):
                    tok = xT[half][:, g * PAIR:(g + 1) * PAIR]
                    MM(bank[4 + half][0:PAIR, g * D:(g + 1) * D], tok, wce[:, :], start=True, stop=True)
                    at = GT + DS * (GP * half + g)
                    MM(bank[7][0:PAIR, at:at + DS], tok, wsp[:, :], start=True, stop=True)
                    last = TP(bank[6][0:PAIR, g * D:(g + 1) * D], tok, ident[:, :])
                last.then_inc(a_done[half], 1)

            def cauchy(k):
                pe.wait_ge(r_ready, k + 1)
                pe.wait_ge(q_ready, k + 1)
                pe.wait_ge(kk_ready, k)
                for i in range(CH):
                    dst = bank[3][0:L, i * 2 * KIND:(i + 1) * 2 * KIND]
                    p = CH * k + i
                    MM(dst, RT[:, i, :], VR[:, p, :], start=True, stop=False)
                    last = MM(dst, QT[:, i, :], VQ[:, p, :], start=False, stop=True)
                last.then_inc(cauchy_done, 1)

            def transpose_norm(k, half):
                pe.wait_ge(xn_ready[half], k + 1)
                if half == 0:
                    pe.wait_ge(xnT_ready[1], k)
                else:
                    pe.wait_ge(xnT_ready[0], k + 1)
                for g in range(GP):
                    last = to_columns(bank[7][:, g * PAIR:(g + 1) * PAIR], xe[half][:, g, :])
                last.then_inc(xnT_done[half], 1)

            def project_out(k, half):
                pe.wait_ge(xnT_ready[half], k + 1)
                pe.wait_ge(mani_read[half], k + 1)
                for g in range(GP):
                    last = MM(bank[4 + half][0:PAIR, g * D:(g + 1) * D], xnT[half][:, g * PAIR:(g + 1) * PAIR], wout[:, :],
                              start=True, stop=True)
                last.then_inc(wout_done[half], 1)

            def tile(k, more):
                for half in range(2):
                    project(k, half)
                for half in range(2):
                    embed(k, half)
                cauchy(k)
                if more:
                    transpose_patches(k + 1)
                else:
                    pe.wait_ge(at_ready, 1)
                    MM(bank[3][0:L, 384:512], dft[:, 0:L], kt[:, 10, :], start=True, stop=False)
                    MM(bank[3][0:L, 384:512], dft[:, L:2 * L], kt[:, 11, :], start=False, stop=True).then_inc(k_T, 1)
                for half in range(2):
                    transpose_norm(k, half)
                for half in range(2):
                    project_out(k, half)

            pe.wait_ge(tok_const, 1)
            pe.wait_ge(s2_ready, 1)
            transpose_patches(0)
            tile(0, True)
            with pe.Fori(1, TILES - 1) as k:
                tile(k, True)
            tile(TILES - 1, False)

            pe.wait_ge(ld_raw, 64)
            for i in range(2 * NX):
                e = i // 2
                if i >= 3:
                    pe.wait_ge(w_lo, i - 2)
                for o in range(FO):
                    src = raw2[:, e, o * 128:(o + 1) * 128] if i % 2 else raw1[:, e * FO + o, :]
                    last = to_columns(bank[i % 3][:, o * 128:(o + 1) * 128], src)
                last.then_inc(w_T, 1)

            pe.wait_ge(ld_toep, 32)
            for half in range(2):
                pe.wait_ge(u_ready[half], TILES)
                pe.wait_ge(h_ready[half], TILES)
                pe.wait_ge(xnT_ready[half], TILES)
                pe.wait_ge(xtok_ready[half], TILES)
            for i in range(D // CONV_H):
                if i >= 4:
                    pe.wait_ge(conv_read, i - 3)
                for c in range(CONV_H):
                    ch = i * CONV_H + c
                    last = MM(bank[4 + i % 4][0:PAIR, c * NPAIR:(c + 1) * NPAIR], Tt[:, :, ch], u[:, :, ch], start=True, stop=True)
                last.then_inc(conv_done, 1)

            def transpose_y(j):
                pe.wait_ge(y_ready, j + 1)
                if j < 4:
                    pe.wait_ge(conv_read, D // CONV_H)
                else:
                    pe.wait_ge(yl_ready, j - 3)
                for g in range(GP):
                    last = to_columns(bank[4 + j % 4][:, g * PAIR:(g + 1) * PAIR], yt[j % 2][:, g, :])
                last.then_inc(y_T, 1)

            def gate(j):
                pe.wait_ge(yl_ready, j + 1)
                for g in range(GP):
                    p = j * GP + g
                    dst = bank[3][0:PAIR, p * E:(p + 1) * E]
                    for n, (a, b) in enumerate(((yh, gwh), (yl, gwh), (yh, gwl), (yl, gwl))):
                        last = MM(dst, a[:, p * PAIR:(p + 1) * PAIR], b[:, :], start=n == 0, stop=n == 3)
                return last

            transpose_y(0)
            for j in range(1, NG):
                transpose_y(j)
                gate(j - 1)
            gate(NG - 1).then_inc(gate_done, 1)
            pe.wait_ge(cw_ready, 1)
            for blk in range(2):
                last = to_columns(bank[7][:, blk * PAIR:(blk + 1) * PAIR],
                                  cw[:, blk * 16:(blk + 1) * 16, :].rearrange("p g e -> p (g e)"))
            last.then_inc(cw_T, 1)
            pe.wait_ge(w_lo, 2 * NX)

            def three(dst, hi_w, lo_w, hi_x, lo_x, start, stop):
                MM(dst, hi_w, hi_x, start=start, stop=False)
                MM(dst, hi_w, lo_x, start=False, stop=False)
                return MM(dst, lo_w, hi_x, start=False, stop=stop)

            def up(c, e, first):
                tok = bass.ds(GT * c, GT)
                for o in range(FO):
                    if not (first and e == 0):
                        pe.wait_ge(act_done, FO * (NX * c + e - 1) + o + 1)
                    blk = slice(o * 128, (o + 1) * 128)
                    three(bank[o][:, 0:GT], w1h[:, e, blk], w1l[:, e, blk], yh[:, tok], yl[:, tok], True, True).then_inc(up_done, 1)

            def down(c, e, first):
                unit = max(e - 1, 0)
                if e != 1 and not (first and unit < 3):
                    pe.wait_ge(scaled, 9 * c + unit - 2)
                for o in range(FO):
                    if o % 2 == 0:
                        pe.wait_ge(split_done, 2 * (NX * c + e) + o // 2 + 1)
                    last = three(bank[4 + unit % 3][:, 0:GT], w2h[:, e, o, :], w2l[:, e, o, :], gh[e % 2][:, o, :], gl[e % 2][:, o, :],
                                 o == 0 and e != 1, o == FO - 1 and e != 0)
                last.then_inc(down_done, 1)

            def output(c):
                pe.wait_ge(added, E * (c + 1))
                pe.wait_ge(out_ready, c)
                for g in range(GP):
                    last = TP(bank[7][0:PAIR, g * D:(g + 1) * D], acc[:, g * PAIR:(g + 1) * PAIR], ident[:, :])
                last.then_inc(out_T, 1)

            def chunk(c, first, last):
                for e in range(NX):
                    if e + 1 < NX:
                        up(c, e + 1, first)
                    elif not last:
                        up(c + 1, 0, False)
                    if e == 1 and not first:
                        output(c - 1)
                    down(c, e, first)

            pe.wait_ge(cwT_ready, 1)
            up(0, 0, True)
            chunk(0, True, False)
            with pe.Fori(1, NG - 1) as c:
                chunk(c, False, False)
            chunk(NG - 1, False, True)
            output(NG - 1)


_INS = ["x", "L0_tok_W_patch", "L0_tok_b_patch", "L0_tok_pos_embed", "L0_tok_W_coord", "L0_tok_b_coord",
        "L0_tok_W_spinor", "L0_tok_b_spinor", "L0_tok_W_embed", "L0_tok_b_embed", "L0_tok_ln_gamma",
        "L0_tok_ln_beta", "L0_tok_W_out", "L0_tok_b_out", "L0_attn_Lambda_re", "L0_attn_Lambda_im",
        "L0_attn_P", "L0_attn_B", "L0_attn_C", "L0_attn_D", "L0_attn_log_step", "L0_ffn_gate_w",
        "L0_ffn_gate_b", "L0_ffn_sw1", "L0_ffn_sb1", "L0_ffn_sw2", "L0_ffn_sb2", "L0_ffn_rw1",
        "L0_ffn_rb1", "L0_ffn_rw2", "L0_ffn_rb2"]


def kernel(**inputs):
    import numpy as _np
    import concourse.bacc as _bacc
    from concourse import mybir as _mybir
    from concourse.bass_utils import run_bass_kernel_spmd as _run

    nc = _bacc.Bacc("TRN2", target_bir_lowering=False, num_devices=1)
    arrays, args = {}, []
    n = _np.arange(L)
    tan = _np.tan(_np.pi * n / L)
    angle = 2 * _np.pi * (n[:, None] * n[None, ::-1] % L) / L
    tables = {
        "ident": _np.eye(128, dtype=_np.float32),
        "tan": _np.stack([2 * tan, tan]).astype(_np.float32),
        "dft": (_np.concatenate([_np.cos(angle), -_np.sin(angle)], 1) / L).astype(_np.float32),
    }
    for name in _INS:
        arrays[f"in_{name}"] = _np.ascontiguousarray(inputs[name])
    for name, a in tables.items():
        arrays[f"table_{name}"] = a
    for name, a in arrays.items():
        args.append(nc.dram_tensor(name, a.shape, _mybir.dt.from_np(a.dtype), kind="ExternalInput").ap())
    args.append(nc.dram_tensor("out", (B, L, D), _mybir.dt.float32, kind="ExternalOutput").ap())
    tower(nc, *args)
    r = _run(nc, [arrays], core_ids=[0])
    return r.results[0]["out"]
```

```python
from contextlib import ExitStack

import concourse.bass as bass
from concourse import mybir

F32 = mybir.dt.float32
F32R = mybir.dt.float32r
ALU = mybir.AluOpType
ACT = mybir.ActivationFunctionType
AX = mybir.AxisListType

B, C, IMG, P = 64, 3, 112, 16
NH = IMG // P
L = NH * NH
D = 128
DC, DS = 8, 4
N = 64
F = 512
FO = F // 128
NS, E = 2, 8
NX = NS + E
T = B * L
PAIR = 2 * L
NPAIR = B // 2
GP = 4
GT = GP * PAIR
NG = T // GT
TILES = 4
TI = B // TILES
TR = TI * NH
HR = TR // 2
KT = C * 2
HP = D // 2
CH = HP // TILES
CONV_H = 16
W_CONV = 2 * NX - D // CONV_H
W_OUT = 3
LN_EPS = 1e-5
KIND = 8
V_BPATCH, V_GAMMA, V_BETA, V_RB2 = 0, 1, 2, 3
V_SB2 = V_RB2 + E
V_B1 = V_SB2 + NS
NV = V_B1 + NX * FO


def tower(nc, x, W_patch, b_patch, pos_embed, W_coord, b_coord, W_spinor, b_spinor, W_embed, b_embed,
          ln_gamma, ln_beta, W_out, b_out, Lambda_re, Lambda_im, P_, B_, C_, D_, log_step,
          gate_w, gate_b, sw1, sb1, sw2, sb2, rw1, rb1, rw2, rb2, c_ident, c_tan, c_dft, out):
    ctx = ExitStack()
    with ctx:
        base = (nc.sbuf_base + 31) // 32 * 32
        end = {}

        def place(name, shape, region, dt=F32):
            size = 4
            for n in shape[1:]:
                size *= n
            at = end[region]
            end[region] = (at + size + 31) // 32 * 32
            return nc.alloc_sbuf_tensor_at(name, shape, dt, offset=at)

        def region(name, start, size):
            end[name] = start
            return start + size

        def sem(name):
            return ctx.enter_context(nc.semaphore(name))

        at = base
        SA, SB_, SC, SH = 4 * F * NX * 4, PAIR * D * 4, 2 * NX * F * 4, NPAIR * D * 4
        region("w", at, SA); at = region("a", at, SA)
        region("y", at, SB_); region("cw", at + 2 * T * 4, 0); region("gt", at + 2 * T * 4 + E * GT * 4, 0); region("b1", at, 0); at = region("b", at, SB_)
        region("su", at, SC); region("cv", at, 0); region("st", at, SC); at = region("g", at, SC)
        at = region("h", at, SH)
        region("o", at, SH); at = region("u", at, SH)
        region("k", at, 0)

        Xc = [place(f"Xc{c}", [TR, P * IMG], "a") for c in range(C)]
        Xr = [place(f"Xr{c}", [TR, NH, P, P], "a") for c in range(C)]
        patchT = place("patchT", [128, KT, NH, TR], "a")
        xT = [place(f"xT{i}", [D, GT], "a") for i in range(2)]
        xtok = [place(f"xtok{i}", [PAIR, GP, D], "a") for i in range(2)]
        xe = xtok
        xnT = [place(f"xnT{i}", [D, GT], "a") for i in range(2)]
        vrows = place("vrows", [NV, D], "su")
        prow = place("prow", [L, D], "su")
        wcrow = place("wcrow", [D, DC], "su")
        wcT = place("wcT", [DC, D], "su")
        we = place("we", [DC, D], "su")
        bccol = place("bccol", [DC, 1], "su")
        gwrow = place("gwrow", [E, D], "su")
        lre = place("lre", [HP, 128], "su")
        lim = place("lim", [HP, 128], "su")
        praw = place("praw", [HP, 128, 2], "su")
        braw = place("braw", [HP, 128, 2], "su")
        craw = place("craw", [HP, 128, 2], "su")
        lsraw = place("lsraw", [HP, 2], "su")
        lsrep = place("lsrep", [HP, 2, N], "su")
        kk = place("kk", [L, D, KIND], "a")
        zeros = place("zeros", [L, D], "su")
        Wp = place("Wp", [128, KT, D], "a")
        wout = place("wout", [D, D], "a")
        wce = place("wce", [D, D], "a")
        assert end["a"] <= end["w"] + SA, (end["a"] - end["w"], SA)
        w1h = place("w1h", [D, NX, F], "w", F32R)
        w1l = place("w1l", [D, NX, F], "w", F32R)
        w2h = place("w2h", [128, NX, FO, D], "w", F32R)
        w2l = place("w2l", [128, NX, FO, D], "w", F32R)
        Tt = place("Tt", [PAIR, PAIR, D], "b")
        yh = place("yh", [D, T], "y", F32R)
        yl = place("yl", [D, T], "y", F32R)
        cwb = place("cwb", [128, E, GT], "cw")
        yt = place("yt", [PAIR, GP, D], "gt")
        y32 = place("y32", [D, GT], "gt")
        lg = place("lg", [PAIR, GP, E], "gt")
        pr = place("pr", [PAIR, GP, E], "gt")
        eq = place("eq", [PAIR, GP, E], "gt")
        rank = place("rank", [PAIR, GP, E], "gt")
        hot = [place(f"hot{i}", [PAIR, GP, E], "gt") for i in range(2)]
        cw = place("cw", [PAIR, GP, E], "gt")
        red = place("red", [PAIR, GP], "gt")
        cwT = place("cwT", [GP * E, PAIR], "gt")
        assert end["gt"] <= end["b"], (end["gt"], end["b"])
        VR = place("VR", [128, HP, 2 * KIND], "b1")
        VQ = place("VQ", [128, HP, 2 * KIND], "b1")
        bT = place("bT", [128, CH, L], "b1")
        dT = place("dT", [128, CH, L], "b1")
        end["kt"] = end["b1"]
        kt = place("kt", [L, 12, D], "kt")
        RT = place("RT", [128, CH, L], "b1")
        QT = place("QT", [128, CH, L], "b1")
        Vr = place("Vr", [128, HP, KIND], "su")
        Vq = place("Vq", [128, HP, KIND], "su")
        prod = place("prod", [128, 14, HP], "su")
        par = place("par", [128, 8, HP], "b1")
        skip = place("skip", [L, D], "b1")
        assert end["b1"] <= end["b"] - SB_ // 2, (end["b1"], end["b"])
        raw1 = place("raw1", [128, NX * FO, D], "st")
        raw2 = place("raw2", [D, NX, F], "st")
        cv = [place(f"cv{i}", [128, 4 * PAIR], "cv") for i in range(2)]
        gf = [place(f"gf{i}", [128, FO, GT], "g") for i in range(2)]
        gh = [place(f"gh{i}", [128, FO, GT], "g", F32R) for i in range(2)]
        gl = [place(f"gl{i}", [128, FO, GT], "g", F32R) for i in range(2)]
        h = place("h", [PAIR, NPAIR, D], "h")
        u = place("u", [PAIR, NPAIR, D], "u")
        acc = place("acc", [D, GT], "o")
        tmp = [place(f"tmp{i}", [D, GT], "o") for i in range(2)]
        osb = place("osb", [PAIR, GP, D], "o")
        ident = place("ident", [128, 128], "k")
        wsp = place("wsp", [D, DS], "k")
        brow = place("brow", [1, 2, D], "su")
        bsp = place("bsp", [PAIR, DS], "k")
        gbb = place("gbb", [PAIR, E], "k")
        gwT = place("gwT", [D, E], "k")
        vcol = place("vcol", [D, NV], "k")
        posb = place("posb", [D, L], "k")
        sb2s = place("sb2s", [D, 1], "k")
        tan2 = place("tan2", [128, L], "k")
        tcol = place("tcol", [L, 1], "k")
        dft = place("dft", [L, 2 * L], "k")
        s2 = place("s2", [128, HP], "k")
        a1 = place("a1", [128, HP], "k")
        a2 = place("a2", [128, HP], "k")
        eps = place("eps", [PAIR, 2 * GP], "k")
        mhalf = place("mhalf", [PAIR, 2 * GP], "k")
        mv = [place(f"mv{i}", [PAIR, 2 * GP, 2], "k") for i in range(2)]
        st = [place(f"st{i}", [PAIR, 2 * GP, 6], "k") for i in range(2)]
        rstd = [place(f"rstd{i}", [PAIR, 2 * GP], "k") for i in range(2)]
        shift = place("shift", [PAIR, GP], "k")
        sp = place("sp", [PAIR, 2 * GP, DS], "k")
        k0 = place("k0", [PAIR, 2 * GP], "k")
        none = place("none", [PAIR, GP], "k")
        ones = place("ones", [1, PAIR], "k", F32R)
        bhi = place("bhi", [1, 2, D], "k", F32R)
        blo = place("blo", [1, 2, D], "k", F32R)
        ksb = place("ksb", [L, D], "k")
        rev = place("rev", [PAIR, E], "k")
        assert end["k"] <= nc.sbuf_usable_end, (end["k"], nc.sbuf_usable_end)
        kpad = nc.dram_tensor("kpad", [2 * L, D], F32).ap()
        cwd = nc.dram_tensor("cwd", [NG, GP, E, PAIR], F32).ap()
        bank = [ctx.enter_context(nc.psum_tensor(f"bank{i}", [128, 512], F32)) for i in range(8)]

        ld_par, ld_tok, ld_vec, ld_wp = sem("ld_par"), sem("ld_tok"), sem("ld_vec"), sem("ld_wp")
        ld_x = [sem(f"ld_x{c}") for c in range(C)]
        ld_raw, ld_toep, ld_skip = sem("ld_raw"), sem("ld_toep"), sem("ld_skip")
        ld_cw = [sem(f"ld_cw{e}") for e in range(E)]
        st_zero, st_k, st_cw, st_out = sem("st_zero"), sem("st_k"), sem("st_cw"), sem("st_out")
        lsrep_ready, par_T, ls_T, vec_T = sem("lsrep_ready"), sem("par_T"), sem("ls_T"), sem("vec_T")
        wcT_ready, wce_T, tok_const, s2_ready = sem("wcT_ready"), sem("wce_T"), sem("tok_const"), sem("s2_ready")
        zero_ready, v_zeroed, pool_const = sem("zero_ready"), sem("v_zeroed"), sem("pool_const")
        bias_ready = sem("bias_ready")
        b_ready, sq_ready, rec_ready, r_ready, q_ready = (sem(n) for n in ("b_ready", "sq_ready", "rec_ready", "r_ready", "q_ready"))
        cauchy_done, kk_ready, at_ready, k_T, k_ready = (sem(n) for n in ("cauchy_done", "kk_ready", "at_ready", "k_T", "k_ready"))
        tp_done = [sem(f"tp_done{i}") for i in range(2)]
        tp_copied = [sem(f"tp_copied{i}") for i in range(2)]
        x_sorted = [sem(f"x_sorted{c}") for c in range(C)]
        proj_done, xT_ready, a_done, mani_read, xtok_ready, xtok_used, xn_ready = (
            [sem(f"{n}{i}") for i in range(2)] for n in
            ("proj_done", "xT_ready", "a_done", "mani_read", "xtok_ready", "xtok_used", "xn_ready"))
        xnT_done, xnT_ready, wout_done, h_ready, u_ready = (
            [sem(f"{n}{i}") for i in range(2)] for n in
            ("xnT_done", "xnT_ready", "wout_done", "h_ready", "u_ready"))
        stats_ready, rstd_ready = ([sem(f"{n}{i}") for i in range(2)] for n in ("stats_ready", "rstd_ready"))
        w_T, w_hi, w_lo = sem("w_T"), sem("w_hi"), sem("w_lo")
        conv_done, conv_copied, conv_T, conv_read = sem("conv_done"), sem("conv_copied"), sem("conv_T"), sem("conv_read")
        stats2, rstd2, y_ready, y_T, yh_ready, yl_ready = (sem(n) for n in ("stats2", "rstd2", "y_ready", "y_T", "yh_ready", "yl_ready"))
        gate_done, lg_ready, exp_ready, cw_ready, cw_T, cwT_ready = (sem(n) for n in ("gate_done", "lg_ready", "exp_ready", "cw_ready", "cw_T", "cwT_ready"))
        up_done, act_done, split_done, down_done = sem("up_done"), sem("act_done"), sem("split_done"), sem("down_done")
        scaled, added, out_T, out_ready = sem("scaled"), sem("added"), sem("out_T"), sem("out_ready")

        block = ctx.enter_context(nc.Block())

        def weights(i, w1, w2):
            return w1[:, i, :] if i < NX else w2[:, i - NX, :, :].rearrange("p o d -> p (o d)")

        def rows(v):
            return v.unsqueeze(0)

        def pairs(k, half):
            return bass.ds(2 * GP * k + GP * half, GP)

        @block.sync
        def _(sp_):
            def load_x(k, c):
                src = x[bass.ds(TI * k, TI), c].rearrange("b (p i) w -> b p (i w)", p=NH)
                sp_.dma_start(Xc[c][:, :], src).then_inc(ld_x[c], 16)

            def load(dst, src, s):
                sp_.dma_start(dst, src).then_inc(s, 16)

            for c in range(C):
                load_x(0, c)
                if c == 0:
                    load(lsraw[:, :], log_step.rearrange("(a b) -> a b", b=2), ld_par)
                    load(Wp[:, :, :], W_patch.rearrange("(t p) d -> p t d", p=128), ld_wp)
            load(tan2[:, :], c_tan[0:1, :].broadcast_to([128, L]), ld_tok)
            load(wsp[:, :], W_spinor, ld_tok)
            load(wout[:, :], W_out, ld_tok)
            load(brow[:, 0, :], rows(b_embed), ld_tok)
            load(brow[:, 1, :], rows(b_out), ld_tok)
            load(bsp[:, :], rows(b_spinor).broadcast_to([PAIR, DS]), ld_tok)
            load(tcol[:, :], c_tan[1, :].unsqueeze(1), ld_tok)
            load(dft[:, :], c_dft, ld_tok)
            load(gbb[:, :], rows(gate_b).broadcast_to([PAIR, E]), ld_tok)
            sp_.wait_ge(zero_ready, 1)
            sp_.dma_start(kpad[L:2 * L, :], zeros[:, :]).then_inc(st_zero, 16)
            sp_.dma_start(skip[L - 1:L, :], D_.unsqueeze(0)).then_inc(ld_skip, 16)
            with sp_.Fori(1, TILES) as k:
                for c in range(C):
                    sp_.wait_ge(x_sorted[c], k)
                    load_x(k, c)
            sp_.wait_ge(bias_ready, 1)
            sp_.wait_ge(st_zero, 16)
            for dst, src in ((raw1[:, 0:NS * FO, :], sw1), (raw1[:, NS * FO:NX * FO, :], rw1)):
                sp_.dma_start(dst, src.rearrange("e (o p) d -> p (e o) d", p=128)).then_inc(ld_raw, 16)
            for dst, src in ((raw2[:, 0:NS, :], sw2), (raw2[:, NS:NX, :], rw2)):
                sp_.dma_start(dst, src.rearrange("e d f -> d e f")).then_inc(ld_raw, 16)
            sp_.wait_ge(st_zero, 16)

            def zero_block(b):
                dst = Tt[(1 - b) * L:(2 - b) * L, b * L:(b + 1) * L, :].rearrange("m l h -> m (l h)")
                sp_.dma_start(dst, kpad[L:2 * L, :].rearrange("l h -> (l h)").unsqueeze(0).broadcast_to([L, L * D])).then_inc(ld_toep, 16)

            zero_block(1)
            sp_.wait_ge(cauchy_done, TILES)
            zero_block(0)
            sp_.wait_ge(k_ready, 1)
            sp_.dma_start(kpad[0:L, :], ksb[:, :]).then_inc(st_k, 16)
            sp_.wait_ge(st_k, 16)
            for b in range(2):
                src = bass.AP(kpad.tensor, (L - 1) * D, [[D, L], [-D, L], [1, D]])
                sp_.dma_start(Tt[b * L:(b + 1) * L, b * L:(b + 1) * L, :], src).then_inc(ld_toep, 16)
            def routing(c, first):
                sp_.wait_ge(cwT_ready, c + 1)
                sp_.dma_start(cwd[bass.ds(c, 1)].rearrange("c g e t -> (c g e) t"), cwT[:, :]).then_inc(st_cw, 16)
                sp_.wait_ge(st_cw, 16 * (c + 1))
                for e in range(E):
                    if not first:
                        sp_.wait_ge(scaled, 9 * (c - 1) + e + 2)
                    src = cwd[bass.ds(c, 1), :, e, :].broadcast_to([128, GP, PAIR])
                    sp_.dma_start(cwb[:, e, :].rearrange("p (g t) -> p g t", g=GP), src).then_inc(ld_cw[e], 16)

            def store(c):
                sp_.wait_ge(out_ready, c + 1)
                dst = out.rearrange("b l d -> (b l) d")[bass.ds(GT * c, GT), :].rearrange("(p i) d -> i p d", p=GP)
                sp_.dma_start(dst, osb[:, :, :]).then_inc(st_out, 16)

            routing(0, True)
            with sp_.Fori(1, NG) as c:
                routing(c, False)
                store(c - 1)
            store(NG - 1)
            sp_.wait_ge(st_out, 16 * NG)

        @block.gpsimd
        def _(pool):
            def load(dst, src):
                pool.dma_start(dst, src).then_inc(ld_vec, 16)

            load(prow[:, :], pos_embed[0])
            for at, src in ((V_BPATCH, rows(b_patch)), (V_GAMMA, rows(ln_gamma)), (V_BETA, rows(ln_beta)), (V_RB2, rb2),
                            (V_SB2, sb2), (V_B1, sb1.rearrange("e (o p) -> (e o) p", p=128)),
                            (V_B1 + NS * FO, rb1.rearrange("e (o p) -> (e o) p", p=128))):
                load(vrows[at:at + src.shape[0], :], src)
            load(wcrow[:, :], W_coord)
            load(gwrow[:, :], gate_w)
            load(we[:, :], W_embed)
            load(bccol[:, :], b_coord.unsqueeze(1))
            nc.gpsimd.memset(skip[:, :], 0.0)
            nc.gpsimd.memset(zeros[:, :], 0.0).then_inc(zero_ready, 1)
            nc.gpsimd.memset(VR[:, :, :], 0.0)
            nc.gpsimd.memset(VQ[:, :, :], 0.0).then_inc(v_zeroed, 1)
            for e in range(E):
                nc.gpsimd.memset(rev[:, e:e + 1], float(E - e))
            nc.gpsimd.memset(none[:, :], 0.0)
            nc.gpsimd.memset(eps[:, :], LN_EPS)
            nc.gpsimd.memset(mhalf[:, :], -0.5).then_inc(pool_const, 1)
            pool.wait_ge(pool_const, 1)

            def inv_std(i, n):
                nc.gpsimd.tensor_tensor(rstd[i][:, 0:n], mv[i][:, 0:n, 1], eps[:, 0:n], ALU.add)
                pool.drain()
                return nc.gpsimd.tensor_tensor(rstd[i][:, 0:n], rstd[i][:, 0:n], mhalf[:, 0:n], ALU.pow)

            for k in range(TILES + 1):
                if k < TILES:
                    pool.wait_ge(rec_ready, k + 1)
                    pool.wait_ge(cauchy_done, k)
                    nc.gpsimd.tensor_tensor(QT[:, :, :], dT[:, :, :], bT[:, :, :], ALU.mult).then_inc(q_ready, 1)
                if k >= 1:
                    pool.wait_ge(stats_ready[1], k)
                    inv_std(1, 2 * GP).then_inc(rstd_ready[1], 1)
                if k < TILES:
                    pool.wait_ge(stats_ready[0], k + 1)
                    inv_std(0, 2 * GP).then_inc(rstd_ready[0], 1)

            def second_norm(c, first):
                pool.wait_ge(stats2, c + 1)
                if not first:
                    pool.wait_ge(y_ready, c)
                inv_std(0, GP)
                pool.drain()
                nc.gpsimd.tensor_tensor(shift[:, :], mv[0][:, 0:GP, 0], rstd[0][:, 0:GP], ALU.mult)
                pool.drain()
                nc.gpsimd.tensor_tensor(shift[:, :], none[:, :], shift[:, :], ALU.subtract).then_inc(rstd2, 1)

            def add_experts(c):
                for e in range(E):
                    pool.wait_ge(scaled, 9 * c + e + 2)
                    nc.gpsimd.tensor_tensor(acc[:, :], acc[:, :], tmp[e % 2][:, :], ALU.add).then_inc(added, 1)
                    pool.drain()

            second_norm(0, True)
            with pool.Fori(0, NG - 1) as c:
                second_norm(c + 1, False)
                add_experts(c)
            add_experts(NG - 1)

        @block.scalar
        def _(act):
            act.dma_start(ident[:, :], c_ident).then_inc(ld_par, 16)
            for dst, src in ((praw, P_), (braw, B_), (craw, C_)):
                act.dma_start(dst[:, :, :], src.rearrange("(a b) n t -> a (b n) t", b=2)).then_inc(ld_par, 16)
            for dst, src in ((lre, Lambda_re), (lim, Lambda_im)):
                act.dma_start(dst[:, :], src.rearrange("(a b) n -> a (b n)", b=2)).then_inc(ld_par, 16)

            def copy_patches(k, t):
                for i, (lo, hi) in enumerate(((0, 4), (4, NH))):
                    act.wait_ge(tp_done[i], KT * k + t + 1)
                    nc.scalar.copy(patchT[:, t, lo:hi, :].rearrange("p w r -> p (w r)"),
                                   bank[i][:, 0:(hi - lo) * TR]).then_inc(tp_copied[i], 1)

            def sort_pixels(k, c):
                act.wait_ge(ld_x[c], 16 * (k + 1))
                nc.scalar.copy(Xr[c][:, :, :, :].rearrange("r w i j -> r i w j"),
                               Xc[c][:, :].rearrange("r (i w j) -> r i w j", i=P, w=NH)).then_inc(x_sorted[c], 1)

            def back(k):
                for half in range(2):
                    act.wait_ge(xnT_done[half], k + 1)
                    nc.scalar.activation(xnT[half][:, :], bank[7 - half][:, 0:GT], ACT.Identity, scale=vcol[:, V_GAMMA:V_GAMMA + 1],
                                         bias=vcol[:, V_BETA:V_BETA + 1]).then_inc(xnT_ready[half], 1)

            def back_out(k):
                for half in range(2):
                    act.wait_ge(wout_done[half], k + 1)
                    nc.scalar.copy(h[:, pairs(k, half), :].rearrange("p g d -> p (g d)"), bank[4 + half][0:PAIR, :]).then_inc(h_ready[half], 1)

            def tile(k, first, more):
                for t in range(KT):
                    copy_patches(k, t)
                    if t == 1:
                        act.wait_ge(b_ready, k + 1)
                        nc.scalar.activation(dT[:, :, :], bT[:, :, :], ACT.Square).then_inc(sq_ready, 1)
                    if t == 3 and not first:
                        back(k - 1)
                    if t == 5 and not first:
                        back_out(k - 1)
                    if t % 2 == 1 and more:
                        sort_pixels(k + 1, t // 2)
                for half in range(2):
                    act.wait_ge(a_done[half], k + 1)
                    nc.scalar.copy(xtok[half][:, :, :].rearrange("p g d -> p (g d)"), bank[6 - 4 * half][0:PAIR, :]).then_inc(xtok_ready[half], 1)
                act.wait_ge(cauchy_done, k + 1)
                nc.scalar.copy(kk[:, bass.ds(2 * CH * k, 2 * CH), :].rearrange("p c v -> p (c v)"),
                               bank[3][0:L, 0:2 * CH * KIND]).then_inc(kk_ready, 1)

            for c in range(C):
                sort_pixels(0, c)
            act.wait_ge(ls_T, 1)
            nc.scalar.activation(s2[:, :], bank[4][:, 0:HP], ACT.Exp, scale=-1.0).then_inc(s2_ready, 1)
            tile(0, True, True)
            with act.Fori(1, TILES - 1) as k:
                tile(k, False, True)
            tile(TILES - 1, False, False)

            def high_weights(lo, hi):
                for i in range(lo, hi):
                    act.wait_ge(w_T, i + 1)
                    nc.scalar.copy(weights(i, w1h, w2h), bank[i % 3][:, :]).then_inc(w_hi, 1)

            high_weights(0, W_OUT)
            act.wait_ge(k_T, 1)
            nc.scalar.copy(ksb[:, :], bank[3][0:L, 384:512]).then_inc(k_ready, 1)
            back(TILES - 1)
            back_out(TILES - 1)
            high_weights(W_OUT, NX)
            act.wait_ge(u_ready[0], TILES)
            act.wait_ge(u_ready[1], TILES)
            high_weights(NX, W_CONV)
            for i in range(D // CONV_H):
                act.wait_ge(conv_done, i + 1)
                if i >= 2:
                    act.wait_ge(conv_T, i - 1)
                nc.scalar.copy(cv[i % 2][:, :], bank[3 + 4 * (i % 2)][:, 0:4 * PAIR]).then_inc(conv_copied, 1)
                high_weights(W_CONV + i, W_CONV + i + 1)

            def norm(c, first):
                act.wait_ge(rstd2, c + 1)
                for g in range(GP):
                    last = nc.scalar.activation(yt[:, g, :], h[:, GP * c + g, :], ACT.Identity,
                                                scale=rstd[0][:, g:g + 1], bias=shift[:, g:g + 1])
                last.then_inc(y_ready, 1)

            def high_y(c, first):
                act.wait_ge(y_T, c + 1)
                if not first:
                    act.wait_ge(gate_done, c)
                    act.wait_ge(yl_ready, c)
                nc.scalar.copy(y32[:, :], bank[7][:, 0:GT])
                nc.scalar.copy(yh[:, bass.ds(GT * c, GT)], bank[7][:, 0:GT]).then_inc(yh_ready, 1)

            def exps(c):
                act.wait_ge(lg_ready, c + 1)
                nc.scalar.activation(pr[:, :, :], lg[:, :, :], ACT.Exp).then_inc(exp_ready, 1)

            def chunk(c, first, last):
                for e in range(NX):
                    if e == 3 and not last:
                        norm(c + 1, False)
                    if e == 5 and not last:
                        high_y(c + 1, False)
                    if e == 7 and not last:
                        exps(c + 1)
                    for o in range(FO):
                        act.wait_ge(up_done, FO * NX * c + FO * e + o + 1)
                        if o == 0 and not (first and e < 2):
                            act.wait_ge(split_done, 2 * (NX * c + e - 1))
                        b1 = vcol[:, V_B1 + FO * e + o:V_B1 + FO * e + o + 1]
                        gelu = nc.scalar.activation(gf[e % 2][:, o, :], bank[o][:, 0:GT], ACT.Gelu, bias=b1)
                        if o == FO - 1:
                            gelu = nc.scalar.activation(gh[e % 2][:, o, :], bank[o][:, 0:GT], ACT.Gelu, bias=b1)
                        gelu.then_inc(act_done, 1)

            norm(0, True)
            high_y(0, True)
            exps(0)
            chunk(0, True, False)
            with act.Fori(1, NG - 1) as c:
                chunk(c, False, False)
            chunk(NG - 1, False, True)

        @block.vector
        def _(dve):
            V = nc.vector
            dve.wait_ge(ld_par, 16 * 7)
            V.tensor_copy(lsrep[:, :, :], lsraw[:, :].unsqueeze(2).broadcast_to([HP, 2, N])).then_inc(lsrep_ready, 1)
            dve.wait_ge(par_T, 1)
            V.tensor_copy(par[:, :, :].rearrange("p a b -> p (a b)"), bank[7][:, :])
            dve.drain()
            Pr, Pi, Br, Bi, Cr, Ci, Lr, Li = (par[:, i, :] for i in range(8))
            V.tensor_scalar(a1[:, :], Lr, -1.0, 1e-4, ALU.mult, ALU.max)
            dve.drain()
            V.tensor_tensor(a2[:, :], a1[:, :], a1[:, :], ALU.mult)

            def over_l(v, k):
                return v[:, bass.ds(CH * k, CH)].unsqueeze(2).broadcast_to([128, CH, L])

            def cauchy_b(k):
                if not isinstance(k, int) or k > 0:
                    dve.wait_ge(q_ready, k)
                V.tensor_tensor(bT[:, :, :], over_l(s2, k), tan2[:, :].unsqueeze(1).broadcast_to([128, CH, L]), ALU.mult)
                dve.drain()
                V.tensor_tensor(bT[:, :, :], bT[:, :, :], over_l(par[:, 7, :], k), ALU.subtract).then_inc(b_ready, 1)

            def cauchy_r(k, first):
                dve.wait_ge(sq_ready, k + 1)
                V.tensor_tensor(dT[:, :, :], dT[:, :, :], over_l(a2, k), ALU.add)
                dve.drain()
                V.reciprocal(dT[:, :, :], dT[:, :, :]).then_inc(rec_ready, 1)
                dve.drain()
                if not first:
                    dve.wait_ge(cauchy_done, k)
                V.tensor_tensor(RT[:, :, :], dT[:, :, :], over_l(a1, k), ALU.mult).then_inc(r_ready, 1)

            def token_stats(i, at, src):
                for g in range(GP):
                    V.bn_stats(st[i][:, at + g, :], src(g))
                dve.drain()
                for g in range(GP):
                    last = V.bn_aggr(mv[i][:, at + g, :], st[i][:, at + g, :])
                return last

            def evacuate_x(k, half, first):
                dve.wait_ge(proj_done[half], k + 1)
                if not first:
                    dve.wait_ge(a_done[half], k)
                V.tensor_tensor(xT[half][:, :].rearrange("p (b h w) -> p b h w", b=HR // NH, h=NH),
                                bank[2 + half][:, 0:GT].rearrange("p (w b h) -> p b h w", w=NH, h=NH),
                                posb[:, :].rearrange("p (h w) -> p h w", h=NH).unsqueeze(1).broadcast_to([D, HR // NH, NH, NH]),
                                ALU.add).then_inc(xT_ready[half], 1)

            def spinors(k):
                dve.wait_ge(a_done[1], k + 1)
                V.tensor_tensor(sp[:, :, :], bank[7][0:PAIR, GT:GT + 2 * GP * DS].rearrange("p (g s) -> p g s", s=DS),
                                bsp[:, :].unsqueeze(1).broadcast_to([PAIR, 2 * GP, DS]), ALU.add)
                dve.drain()
                V.tensor_tensor(sp[:, :, :], sp[:, :, :], sp[:, :, :], ALU.mult)
                dve.drain()
                V.tensor_reduce(k0[:, :], sp[:, :, :], AX.X, ALU.add)
                dve.drain()

            def enhance(k, half):
                dve.wait_ge(xtok_ready[half], k + 1)
                for g in range(GP):
                    last = V.scalar_tensor_tensor(xe[half][:, g, :], bank[4 + half][0:PAIR, g * D:(g + 1) * D],
                                                  k0[:, GP * half + g:GP * half + g + 1], xtok[half][:, g, :], ALU.mult, ALU.add)
                last.then_inc(xtok_used[half], 1)
                dve.drain()
                last = token_stats(0, GP * half, lambda g: xe[half][:, g, :])
                if half == 1:
                    last.then_inc(stats_ready[0], 1)

            def first_norm(k):
                dve.wait_ge(rstd_ready[0], k + 1)
                for half in range(2):
                    for g in range(GP):
                        n = GP * half + g
                        last = V.tensor_scalar(xe[half][:, g, :], xe[half][:, g, :], mv[0][:, n, 0:1], rstd[0][:, n:n + 1],
                                               ALU.subtract, ALU.mult)
                    last.then_inc(xn_ready[half], 1)

            def output_stats(k):
                for half in range(2):
                    dve.wait_ge(h_ready[half], k + 1)
                    last = token_stats(1, GP * half, lambda g: h[:, 2 * GP * k + GP * half + g, :])
                last.then_inc(stats_ready[1], 1)

            def conv_input(k):
                dve.wait_ge(rstd_ready[1], k + 1)
                for half in range(2):
                    for g in range(GP):
                        n = GP * half + g
                        p = 2 * GP * k + n
                        last = V.tensor_scalar(u[:, p, :], h[:, p, :], mv[1][:, n, 0:1], rstd[1][:, n:n + 1], ALU.subtract, ALU.mult)
                    last.then_inc(u_ready[half], 1)

            def at_roots():
                dve.wait_ge(kk_ready, TILES)
                r00, i00, r01, i01, r10, i10, r11, i11 = (kk[:, :, i] for i in range(KIND))
                t = [kt[:, i, :] for i in range(12)]

                def tt(o, a, b, op):
                    V.tensor_tensor(t[o], a, b, op)

                tt(0, r01, r10, ALU.mult); tt(1, i01, i10, ALU.mult); tt(2, r01, i10, ALU.mult); tt(3, i01, r10, ALU.mult)
                V.tensor_scalar(t[4], r11, 1.0, None, ALU.add); tt(5, i11, i11, ALU.mult)
                dve.drain()
                tt(6, t[0], t[1], ALU.subtract); tt(7, t[2], t[3], ALU.add); tt(8, t[4], t[4], ALU.mult)
                dve.drain()
                tt(8, t[8], t[5], ALU.add); tt(0, t[6], t[4], ALU.mult); tt(1, t[7], i11, ALU.mult)
                tt(2, t[7], t[4], ALU.mult); tt(3, t[6], i11, ALU.mult)
                dve.drain()
                V.reciprocal(t[8], t[8]); tt(0, t[0], t[1], ALU.add); tt(2, t[2], t[3], ALU.subtract)
                dve.drain()
                tt(0, t[0], t[8], ALU.mult); tt(2, t[2], t[8], ALU.mult)
                dve.drain()
                tt(0, r00, t[0], ALU.subtract); tt(2, i00, t[2], ALU.subtract)
                dve.drain()
                V.tensor_scalar(t[1], t[2], tcol[:, 0:1], None, ALU.mult); V.tensor_scalar(t[3], t[0], tcol[:, 0:1], None, ALU.mult)
                dve.drain()
                tt(10, t[0], t[1], ALU.subtract)
                V.tensor_tensor(t[11], t[2], t[3], ALU.add).then_inc(at_ready, 1)

            def low_weights(lo, hi):
                for i in range(lo, hi):
                    dve.wait_ge(w_hi, i + 1)
                    V.tensor_tensor(weights(i, w1l, w2l), bank[i % 3][:, :], weights(i, w1h, w2h).bitcast(F32),
                                    ALU.subtract).then_inc(w_lo, 1)

            def tile(k, first, more):
                if not first:
                    first_norm(k - 1)
                    cauchy_r(k, first)
                if not first:
                    output_stats(k - 1)
                for half in range(2):
                    evacuate_x(k, half, first)
                spinors(k)
                for half in range(2):
                    enhance(k, half)
                if more:
                    cauchy_b(k + 1)
                if not more:
                    at_roots()
                    first_norm(k)
                    low_weights(0, W_OUT)
                if not first:
                    conv_input(k - 1)
                dve.drain()

            dve.wait_ge(s2_ready, 1)
            dve.wait_ge(ld_tok, 16 * 9)
            dve.drain()
            cauchy_b(0)
            products = [(Cr, Br), (Ci, Bi), (Cr, Bi), (Ci, Br), (Cr, Pr), (Ci, Pi), (Cr, Pi), (Ci, Pr),
                        (Pr, Br), (Pi, Bi), (Pr, Bi), (Pi, Br), (Pr, Pr), (Pi, Pi)]
            for i, (p, q) in enumerate(products):
                V.tensor_tensor(prod[:, i, :], p, q, ALU.mult)
            V.memset(Vr[:, :, KIND - 1], 0.0)
            dve.drain()
            for i in range(7):
                V.tensor_tensor(Vr[:, :, i], prod[:, 2 * i, :], prod[:, 2 * i + 1, :], ALU.subtract if i in (1, 3, 5) else ALU.add)
            dve.drain()
            cauchy_r(0, True)
            V.tensor_copy(Vq[:, :, 0:KIND:2], Vr[:, :, 1:KIND:2])
            V.tensor_scalar(Vq[:, :, 1:KIND:2], Vr[:, :, 0:KIND:2], -1.0, None, ALU.mult)
            dve.drain()
            dve.wait_ge(v_zeroed, 1)
            for b in range(2):
                rows_ = slice(64 * b, 64 * b + 64)
                V.tensor_copy(VR[rows_, :, KIND * b:KIND * (b + 1)], Vr[rows_, :, :])
                V.tensor_copy(VQ[rows_, :, KIND * b:KIND * (b + 1)], Vq[rows_, :, :])
            dve.wait_ge(vec_T, 1)
            dve.wait_ge(ld_vec, 16 * 12)
            V.tensor_copy(vcol[:, :], bank[5][:, 0:NV])
            V.tensor_copy(wcT[:, :], bank[5][0:DC, 128:256])
            V.tensor_copy(gwT[:, :], bank[5][:, 256:256 + E]).then_inc(wcT_ready, 1)
            dve.drain()
            V.tensor_scalar(posb[:, :], bank[5][:, 64:64 + L], vcol[:, V_BPATCH:V_BPATCH + 1], None, ALU.add)
            V.tensor_tensor(sb2s[:, :], vcol[:, V_SB2:V_SB2 + 1], vcol[:, V_SB2 + 1:V_SB2 + 2], ALU.add)
            dve.wait_ge(wce_T, 1)
            V.tensor_copy(wce[:, :], bank[6][:, 0:D])
            V.memset(ones[:, :].bitcast(F32), 1.0)
            V.tensor_tensor(brow[:, 0, :], brow[:, 0, :], bank[6][0:1, D:2 * D], ALU.add).then_inc(tok_const, 1)
            dve.drain()
            V.tensor_copy(bhi[:, :, :], brow[:, :, :])
            dve.drain()
            V.tensor_tensor(blo[:, :, :], brow[:, :, :], bhi[:, :, :].bitcast(F32), ALU.subtract).then_inc(bias_ready, 1)
            dve.wait_ge(pool_const, 1)
            dve.drain()
            tile(0, True, True)
            with dve.Fori(1, TILES - 1) as k:
                tile(k, False, True)
            tile(TILES - 1, False, False)

            output_stats(TILES - 1)
            low_weights(W_OUT, W_OUT + 3)
            conv_input(TILES - 1)
            low_weights(W_OUT + 3, W_CONV)
            for i in range(D // CONV_H):
                low_weights(W_CONV + i, W_CONV + i + 1)
                dve.wait_ge(conv_T, i + 1)
                part = h[:, :, i * CONV_H:(i + 1) * CONV_H]
                V.tensor_tensor(part, part, bank[4 + i % 3][0:PAIR, :].rearrange("p (c g) -> p g c", c=CONV_H),
                                ALU.add).then_inc(conv_read, 1)
            dve.drain()

            def second_stats(c, first):
                if not first:
                    dve.wait_ge(y_ready, c)
                token_stats(0, 0, lambda g: h[:, GP * c + g, :]).then_inc(stats2, 1)

            def low_y(c):
                dve.wait_ge(yh_ready, c + 1)
                span = bass.ds(GT * c, GT)
                V.tensor_tensor(yl[:, span], y32[:, :], yh[:, span].bitcast(F32), ALU.subtract).then_inc(yl_ready, 1)

            def split(c, e, first):
                for p in range(2):
                    dve.wait_ge(act_done, FO * NX * c + FO * e + 2 * p + 2)
                    if p == 0 and not (first and e < 2):
                        dve.wait_ge(down_done, NX * c + e - 1)
                    span = slice(2 * p, 2 * p + 2)
                    own = slice(2 * p, 2 * p + 2 - p)
                    V.tensor_copy(gh[e % 2][:, own, :], gf[e % 2][:, own, :])
                    dve.drain()
                    V.tensor_tensor(gl[e % 2][:, span, :], gf[e % 2][:, span, :], gh[e % 2][:, span, :].bitcast(F32),
                                    ALU.subtract).then_inc(split_done, 1)

            def wide(v):
                return v[:, :].unsqueeze(2).broadcast_to([PAIR, GP, E])

            def gate_logits(c):
                dve.wait_ge(gate_done, c + 1)
                V.tensor_tensor(lg[:, :, :], bank[7][0:PAIR, 0:GP * E].rearrange("p (g e) -> p g e", e=E),
                                gbb[:, :].unsqueeze(1).broadcast_to([PAIR, GP, E]), ALU.add)
                dve.drain()
                V.tensor_reduce(red[:, :], lg[:, :, :], AX.X, ALU.max)
                dve.drain()
                V.tensor_tensor(lg[:, :, :], lg[:, :, :], wide(red), ALU.subtract).then_inc(lg_ready, 1)

            def rank_highest(src):
                V.tensor_reduce(red[:, :], src[:, :, :], AX.X, ALU.max)
                dve.drain()
                V.tensor_tensor(eq[:, :, :], src[:, :, :], wide(red), ALU.is_equal)
                dve.drain()
                V.tensor_tensor(rank[:, :, :], eq[:, :, :], rev[:, :].unsqueeze(1).broadcast_to([PAIR, GP, E]), ALU.mult)
                dve.drain()

            def pick_first(n):
                V.tensor_reduce(red[:, :], rank[:, :, :], AX.X, ALU.max)
                dve.drain()
                V.tensor_tensor(hot[n][:, :, :], rank[:, :, :], wide(red), ALU.is_equal)
                dve.drain()

            def gate_probs(c):
                dve.wait_ge(exp_ready, c + 1)
                V.tensor_reduce(red[:, :], pr[:, :, :], AX.X, ALU.add)
                dve.drain()
                V.reciprocal(red[:, :], red[:, :])
                dve.drain()
                V.tensor_tensor(pr[:, :, :], pr[:, :, :], wide(red), ALU.mult)
                dve.drain()
                rank_highest(pr)

            def gate_second():
                pick_first(0)
                V.scalar_tensor_tensor(lg[:, :, :], hot[0][:, :, :], -2.0, pr[:, :, :], ALU.mult, ALU.add)
                dve.drain()
                rank_highest(lg)

            def gate_weights():
                pick_first(1)
                V.tensor_tensor(eq[:, :, :], hot[0][:, :, :], hot[1][:, :, :], ALU.add)
                dve.drain()
                V.tensor_tensor(cw[:, :, :], eq[:, :, :], pr[:, :, :], ALU.mult).then_inc(cw_ready, 1)

            def gate_rows(c, first):
                dve.wait_ge(cw_T, c + 1)
                if not first:
                    dve.wait_ge(st_cw, 16 * c)
                V.tensor_copy(cwT[:, :], bank[7][0:GP * E, 0:PAIR]).then_inc(cwT_ready, 1)

            def combine(c, unit, first):
                src = bank[4 + unit % 3][:, 0:GT]
                dve.wait_ge(down_done, NX * c + unit + 2)
                if unit == 0:
                    if not first:
                        dve.wait_ge(out_T, c)
                    V.tensor_scalar(acc[:, :], src, sb2s[:, 0:1], None, ALU.add).then_inc(scaled, 1)
                    return
                e = unit - 1
                dve.wait_ge(ld_cw[e], 16 * (c + 1))
                if not (first and e < 2):
                    dve.wait_ge(added, E * c + e - 1)
                V.scalar_tensor_tensor(tmp[e % 2][:, :], src, vcol[:, V_RB2 + e:V_RB2 + e + 1], cwb[:, e, :],
                                       ALU.add, ALU.mult).then_inc(scaled, 1)

            def output(c, first):
                dve.wait_ge(out_T, c + 1)
                if not first:
                    dve.wait_ge(st_out, 16 * c)
                V.tensor_tensor(osb[:, :, :], bank[7][0:PAIR, :].rearrange("p (g d) -> p g d", g=GP),
                                h[:, bass.ds(GP * c, GP), :], ALU.add).then_inc(out_ready, 1)

            def chunk(c, first, second, last):
                for e in range(NX):
                    split(c, e, first)
                    if e == 0 and first:
                        gate_probs(0)
                        gate_second()
                        gate_weights()
                    if e == 1 and first:
                        gate_rows(0, True)
                    if e == 0 and not first:
                        combine(c - 1, NX - 2, second)
                    if e == 2 and not first:
                        output(c - 1, second)
                    if e >= 2:
                        combine(c, e - 2, first)
                    if not last:
                        if e == 0:
                            second_stats(c + 1, False)
                        if e == 4:
                            low_y(c + 1)
                        if e == 5:
                            gate_logits(c + 1)
                        if e == 6:
                            gate_probs(c + 1)
                        if e == 7:
                            gate_second()
                        if e == 8:
                            gate_weights()
                        if e == 9:
                            gate_rows(c + 1, False)

            second_stats(0, True)
            low_y(0)
            gate_logits(0)
            chunk(0, True, False, False)
            chunk(1, False, True, False)
            with dve.Fori(2, NG - 1) as c:
                chunk(c, False, False, False)
            chunk(NG - 1, False, False, True)
            combine(NG - 1, NX - 2, False)
            output(NG - 1, False)

        @block.tensor
        def _(pe):
            MM, TP = nc.tensor.matmul, nc.tensor.transpose

            def to_columns(dst, src):
                rows_ = src.shape[0]
                return TP(dst, src, ident[0:rows_, 0:rows_])

            pe.wait_ge(ld_par, 16 * 7)
            for i, src in enumerate((praw[:, :, 0], praw[:, :, 1], braw[:, :, 0], braw[:, :, 1], craw[:, :, 0], craw[:, :, 1],
                                     lre[:, :], lim[:, :])):
                last = to_columns(bank[7][:, i * HP:(i + 1) * HP], src)
            last.then_inc(par_T, 1)
            pe.wait_ge(lsrep_ready, 1)
            to_columns(bank[4][:, 0:HP], lsrep[:, :, :].rearrange("p b n -> p (b n)")).then_inc(ls_T, 1)
            def transpose_patches(k, t, first):
                c, top = t // 2, t % 2
                if top == 0:
                    pe.wait_ge(x_sorted[c], k + 1)
                src = Xr[c][:, :, top * 8:top * 8 + 8, :].rearrange("r w i j -> r w (i j)")
                for i, (lo, hi) in enumerate(((0, 4), (4, NH))):
                    if not (first and t == 0):
                        pe.wait_ge(tp_copied[i], KT * k + t)
                    for w in range(lo, hi):
                        last = to_columns(bank[i][:, (w - lo) * TR:(w - lo + 1) * TR], src[:, w, :])
                    last.then_inc(tp_done[i], 1)

            def project(k, t, first):
                for i in range(2):
                    pe.wait_ge(tp_copied[i], KT * k + t + 1)
                if t == 0 and not first:
                    pe.wait_ge(xtok_ready[1], k)
                    pe.wait_ge(kk_ready, k)
                for half in range(2):
                    last = MM(bank[2 + half][:, 0:GT], Wp[:, t, :], patchT[:, t, :, half * HR:(half + 1) * HR],
                              start=t == 0, stop=t == KT - 1)
                    if t == KT - 1:
                        last.then_inc(proj_done[half], 1)

            def add_bias(dst, i):
                for n, part in enumerate((bhi, blo)):
                    MM(dst[0:PAIR, :], ones[:, :], part[:, i, :].unsqueeze(1).broadcast_to([1, GP, D]), start=n == 0, stop=False)

            def embed(k, half, first):
                pe.wait_ge(xT_ready[half], k + 1)
                if not first:
                    pe.wait_ge(h_ready[half], k)
                    pe.wait_ge(xnT_ready[half], k)
                add_bias(bank[4 + half], 0)
                for g in range(GP):
                    tok = xT[half][:, g * PAIR:(g + 1) * PAIR]
                    MM(bank[4 + half][0:PAIR, g * D:(g + 1) * D], tok, wce[:, :], start=False, stop=g == GP - 1)
                    at = GT + DS * (GP * half + g)
                    MM(bank[7][0:PAIR, at:at + DS], tok, wsp[:, :], start=True, stop=True)
                    last = TP(bank[6 - 4 * half][0:PAIR, g * D:(g + 1) * D], tok, ident[:, :])
                last.then_inc(a_done[half], 1)

            def cauchy(k):
                pe.wait_ge(r_ready, k + 1)
                pe.wait_ge(q_ready, k + 1)
                for i in range(CH):
                    dst = bank[3][0:L, i * 2 * KIND:(i + 1) * 2 * KIND]
                    p = CH * k + i
                    MM(dst, RT[:, i, :], VR[:, p, :], start=True, stop=False)
                    last = MM(dst, QT[:, i, :], VQ[:, p, :], start=False, stop=True)
                last.then_inc(cauchy_done, 1)

            def transpose_norm(k, half):
                pe.wait_ge(xn_ready[half], k + 1)
                if half == 1:
                    pe.wait_ge(xtok_ready[0], k + 1)
                for g in range(GP):
                    last = to_columns(bank[7 - half][:, g * PAIR:(g + 1) * PAIR], xe[half][:, g, :])
                last.then_inc(xnT_done[half], 1)

            def project_out(k, half):
                pe.wait_ge(xnT_ready[half], k + 1)
                pe.wait_ge(xtok_used[half], k + 1)
                add_bias(bank[4 + half], 1)
                for g in range(GP):
                    last = MM(bank[4 + half][0:PAIR, g * D:(g + 1) * D], xnT[half][:, g * PAIR:(g + 1) * PAIR], wout[:, :],
                              start=False, stop=g == GP - 1)
                last.then_inc(wout_done[half], 1)

            def tile(k, first):
                for t in range(KT):
                    transpose_patches(k, t, first)
                    if t == 0 and first:
                        pe.wait_ge(ld_wp, 16)
                    if t >= 1:
                        project(k, t - 1, first)
                    if t == 3 and first:
                        pe.wait_ge(ld_vec, 16 * 12)
                        to_columns(bank[5][:, 0:NV], vrows[:, :])
                        to_columns(bank[5][:, 64:64 + L], prow[:, :])
                        to_columns(bank[5][0:DC, 128:256], wcrow[:, :])
                        to_columns(bank[5][:, 256:256 + E], gwrow[:, :]).then_inc(vec_T, 1)
                    if t == 3 and not first:
                        for half in range(2):
                            transpose_norm(k - 1, half)
                    if t == 5 and not first:
                        for half in range(2):
                            project_out(k - 1, half)
                project(k, KT - 1, first)
                if first:
                    pe.wait_ge(wcT_ready, 1)
                    MM(bank[6][:, 0:D], wcT[:, :], we[:, :], start=True, stop=True)
                    MM(bank[6][0:1, D:2 * D], bccol[:, :], we[:, :], start=True, stop=True).then_inc(wce_T, 1)
                    pe.wait_ge(tok_const, 1)
                    pe.wait_ge(bias_ready, 1)
                for half in range(2):
                    embed(k, half, first)
                cauchy(k)

            tile(0, True)
            with pe.Fori(1, TILES) as k:
                tile(k, False)

            def transpose_weights(lo, hi):
                for i in range(lo, hi):
                    if i >= 3:
                        pe.wait_ge(w_lo, i - 2)
                    for o in range(FO):
                        src = raw1[:, i * FO + o, :] if i < NX else raw2[:, i - NX, o * 128:(o + 1) * 128]
                        last = to_columns(bank[i % 3][:, o * 128:(o + 1) * 128], src)
                    last.then_inc(w_T, 1)

            def convolve(i):
                if i >= 2:
                    pe.wait_ge(conv_copied, i - 1)
                for c in range(CONV_H):
                    slot, quarter = c // 4, c % 4
                    last = MM(bank[3 + 4 * (i % 2)][quarter * NPAIR:(quarter + 1) * NPAIR, slot * PAIR:(slot + 1) * PAIR],
                              u[:, :, i * CONV_H + c], Tt[:, :, i * CONV_H + c], start=True, stop=True,
                              tile_position=(0, quarter * NPAIR))
                last.then_inc(conv_done, 1)

            def transpose_conv(i):
                pe.wait_ge(conv_copied, i + 1)
                if i >= 3:
                    pe.wait_ge(conv_read, i - 2)
                for slot in range(4):
                    last = to_columns(bank[4 + i % 3][0:PAIR, slot * 128:(slot + 1) * 128], cv[i % 2][:, slot * PAIR:(slot + 1) * PAIR])
                last.then_inc(conv_T, 1)

            pe.wait_ge(ld_raw, 64)
            pe.wait_ge(xtok_ready[1], TILES)
            transpose_weights(0, W_OUT)
            pe.wait_ge(ld_skip, 16)
            pe.wait_ge(at_ready, 1)
            MM(bank[3][0:L, 384:512], dft[:, 0:L], kt[:, 10, :], start=True, stop=False)
            MM(bank[3][0:L, 384:512], dft[:, L:2 * L], kt[:, 11, :], start=False, stop=False)
            MM(bank[3][0:L, 384:512], ident[0:L, 0:L], skip[:, :], start=False, stop=True).then_inc(k_T, 1)
            for half in range(2):
                transpose_norm(TILES - 1, half)
            for half in range(2):
                project_out(TILES - 1, half)
            transpose_weights(W_OUT, W_CONV)
            pe.wait_ge(ld_toep, 64)
            for half in range(2):
                pe.wait_ge(u_ready[half], TILES)
                pe.wait_ge(h_ready[half], TILES)
                pe.wait_ge(xnT_ready[half], TILES)
            for i in range(D // CONV_H):
                convolve(i)
                transpose_weights(W_CONV + i, W_CONV + i + 1)
                if i >= 1:
                    transpose_conv(i - 1)
            transpose_conv(D // CONV_H - 1)

            def transpose_y(c, first):
                pe.wait_ge(y_ready, c + 1)
                if first:
                    pe.wait_ge(conv_read, D // CONV_H)
                for g in range(GP):
                    last = to_columns(bank[7][:, g * PAIR:(g + 1) * PAIR], yt[:, g, :])
                last.then_inc(y_T, 1)

            def gate(c):
                pe.wait_ge(yh_ready, c + 1)
                for g in range(GP):
                    last = MM(bank[7][0:PAIR, g * E:(g + 1) * E], y32[:, g * PAIR:(g + 1) * PAIR], gwT[:, :], start=True, stop=True)
                last.then_inc(gate_done, 1)

            def transpose_cw(c):
                pe.wait_ge(cw_ready, c + 1)
                to_columns(bank[7][0:GP * E, 0:PAIR], cw[:, :, :].rearrange("p g e -> p (g e)")).then_inc(cw_T, 1)

            def three(dst, hi_w, lo_w, hi_x, lo_x, start, stop):
                MM(dst, hi_w, hi_x, start=start, stop=False)
                MM(dst, hi_w, lo_x, start=False, stop=False)
                return MM(dst, lo_w, hi_x, start=False, stop=stop)

            def up(c, e, first):
                tok = bass.ds(GT * c, GT)
                for o in range(FO):
                    if not (first and e == 0):
                        pe.wait_ge(act_done, FO * (NX * c + e - 1) + o + 1)
                    blk = slice(o * 128, (o + 1) * 128)
                    three(bank[o][:, 0:GT], w1h[:, e, blk], w1l[:, e, blk], yh[:, tok], yl[:, tok], True, True).then_inc(up_done, 1)

            def down(c, e, first):
                unit = max(e - 1, 0)
                if e != 1 and not (first and unit < 3):
                    pe.wait_ge(scaled, 9 * c + unit - 2)
                for o in range(FO):
                    if o % 2 == 0:
                        pe.wait_ge(split_done, 2 * (NX * c + e) + o // 2 + 1)
                    last = three(bank[4 + unit % 3][:, 0:GT], w2h[:, e, o, :], w2l[:, e, o, :], gh[e % 2][:, o, :], gl[e % 2][:, o, :],
                                 o == 0 and e != 1, o == FO - 1 and e != 0)
                last.then_inc(down_done, 1)

            def output(c, last):
                pe.wait_ge(added, E * (c + 1))
                if not last:
                    pe.wait_ge(cwT_ready, c + 2)
                for g in range(GP):
                    last = TP(bank[7][0:PAIR, g * D:(g + 1) * D], acc[:, g * PAIR:(g + 1) * PAIR], ident[:, :])
                last.then_inc(out_T, 1)

            def chunk(c, first, last):
                for e in range(NX):
                    if e + 1 < NX:
                        up(c, e + 1, first)
                    elif not last:
                        pe.wait_ge(yl_ready, c + 2)
                        up(c + 1, 0, False)
                    if e == 1:
                        transpose_cw(0) if first else output(c - 1, False)
                    if not last:
                        if e == 3:
                            if not first:
                                pe.wait_ge(out_ready, c)
                            transpose_y(c + 1, False)
                        if e == 4:
                            gate(c + 1)
                        if e == 9:
                            transpose_cw(c + 1)
                    down(c, e, first)

            transpose_y(0, True)
            gate(0)
            pe.wait_ge(w_lo, 2 * NX)
            pe.wait_ge(yl_ready, 1)
            up(0, 0, True)
            chunk(0, True, False)
            with pe.Fori(1, NG - 1) as c:
                chunk(c, False, False)
            chunk(NG - 1, False, True)
            pe.wait_ge(out_ready, NG - 1)
            output(NG - 1, True)


_INS = ["x", "L0_tok_W_patch", "L0_tok_b_patch", "L0_tok_pos_embed", "L0_tok_W_coord", "L0_tok_b_coord",
        "L0_tok_W_spinor", "L0_tok_b_spinor", "L0_tok_W_embed", "L0_tok_b_embed", "L0_tok_ln_gamma",
        "L0_tok_ln_beta", "L0_tok_W_out", "L0_tok_b_out", "L0_attn_Lambda_re", "L0_attn_Lambda_im",
        "L0_attn_P", "L0_attn_B", "L0_attn_C", "L0_attn_D", "L0_attn_log_step", "L0_ffn_gate_w",
        "L0_ffn_gate_b", "L0_ffn_sw1", "L0_ffn_sb1", "L0_ffn_sw2", "L0_ffn_sb2", "L0_ffn_rw1",
        "L0_ffn_rb1", "L0_ffn_rw2", "L0_ffn_rb2"]


def kernel(**inputs):
    import numpy as _np
    import concourse.bacc as _bacc
    from concourse import mybir as _mybir
    from concourse.bass_utils import run_bass_kernel_spmd as _run

    nc = _bacc.Bacc("TRN2", target_bir_lowering=False, num_devices=1)
    arrays, args = {}, []
    n = _np.arange(L)
    tan = _np.tan(_np.pi * n / L)
    angle = 2 * _np.pi * (n[:, None] * n[None, ::-1] % L) / L
    tables = {
        "ident": _np.eye(128, dtype=_np.float32),
        "tan": _np.stack([2 * tan, tan]).astype(_np.float32),
        "dft": (_np.concatenate([_np.cos(angle), -_np.sin(angle)], 1) / L).astype(_np.float32),
    }
    for name in _INS:
        arrays[f"in_{name}"] = _np.ascontiguousarray(inputs[name])
    for name, a in tables.items():
        arrays[f"table_{name}"] = a
    for name, a in arrays.items():
        args.append(nc.dram_tensor(name, a.shape, _mybir.dt.from_np(a.dtype), kind="ExternalInput").ap())
    args.append(nc.dram_tensor("out", (B, L, D), _mybir.dt.float32, kind="ExternalOutput").ap())
    tower(nc, *args)
    r = _run(nc, [arrays], core_ids=[0])
    return r.results[0]["out"]
```

```python
from contextlib import ExitStack

import concourse.bass as bass
from concourse import mybir

F32 = mybir.dt.float32
F32R = mybir.dt.float32r
ALU = mybir.AluOpType
ACT = mybir.ActivationFunctionType
AX = mybir.AxisListType

B, C, IMG, P = 64, 3, 112, 16
NH = IMG // P
L = NH * NH
D = 128
DC, DS = 8, 4
N = 64
F = 512
FO = F // 128
NS, E = 2, 8
NX = NS + E
T = B * L
PAIR = 2 * L
NPAIR = B // 2
GP = 4
GT = GP * PAIR
NG = T // GT
TILES = 4
TI = B // TILES
TR = TI * NH
HR = TR // 2
KT = C * 2
HP = D // 2
CH = HP // TILES
CONV_H = 16
CONVS = D // CONV_H
HB = 4
HALF = HB // 2
W_OUT = 3
W_CONV = 12
W_END = 17
LN_EPS = 1e-5
KIND = 8
V_BPATCH, V_GAMMA, V_BETA, V_RB2 = 0, 1, 2, 3
V_SB2 = V_RB2 + E
V_B1 = V_SB2 + NS
NV = V_B1 + NX * FO


def tower(nc, x, W_patch, b_patch, pos_embed, W_coord, b_coord, W_spinor, b_spinor, W_embed, b_embed,
          ln_gamma, ln_beta, W_out, b_out, Lambda_re, Lambda_im, P_, B_, C_, D_, log_step,
          gate_w, gate_b, sw1, sb1, sw2, sb2, rw1, rb1, rw2, rb2, c_ident, c_tan, c_dft, out):
    ctx = ExitStack()
    with ctx:
        base = (nc.sbuf_base + 31) // 32 * 32
        end = {}

        def place(name, shape, region, dt=F32):
            size = 4
            for n in shape[1:]:
                size *= n
            at = end[region]
            end[region] = (at + size + 31) // 32 * 32
            return nc.alloc_sbuf_tensor_at(name, shape, dt, offset=at)

        def region(name, start, size):
            end[name] = start
            return start + size

        def sem(name):
            return ctx.enter_context(nc.semaphore(name))

        at = base
        SA, SB_, SC, SH = 4 * F * NX * 4, PAIR * D * 4, 2 * NX * F * 4, NPAIR * D * 4
        region("w", at, SA); at = region("a", at, SA)
        region("y", at, SB_); region("cw", at + 2 * T * 4, 0); region("gt", at + 2 * T * 4 + E * GT * 4, 0)
        region("b1", at, 0); at = region("b", at, SB_)
        region("su", at, SC); region("cv", at, 0); region("st", at, SC); at = region("g", at, SC)
        at = region("h", at, SH)
        region("o", at, SH); at = region("u", at, SH)
        region("k", at, 0)

        Xc = [place(f"Xc{c}", [TR, P * IMG], "a") for c in range(C)]
        Xr = [place(f"Xr{c}", [TR, NH, P, P], "a") for c in range(C)]
        patchT = place("patchT", [128, KT, NH, TR], "a")
        xT = [place(f"xT{i}", [D, GT], "a") for i in range(2)]
        xtok = [place(f"xtok{i}", [PAIR, GP, D], "a") for i in range(2)]
        xe = xtok
        xnT = [place(f"xnT{i}", [D, GT], "a") for i in range(2)]
        vrows = place("vrows", [NV, D], "su")
        prow = place("prow", [L, D], "su")
        wcrow = place("wcrow", [D, DC], "su")
        wcT = place("wcT", [DC, D], "su")
        we = place("we", [DC, D], "su")
        bccol = place("bccol", [DC, 1], "su")
        gwrow = place("gwrow", [E, D], "su")
        lre = place("lre", [HP, 128], "su")
        lim = place("lim", [HP, 128], "su")
        praw = place("praw", [HP, 128, 2], "su")
        braw = place("braw", [HP, 128, 2], "su")
        craw = place("craw", [HP, 128, 2], "su")
        lsraw = place("lsraw", [HP, 2], "su")
        lsrep = place("lsrep", [HP, 2, N], "su")
        kk = place("kk", [L, D, KIND], "a")
        kf = place("kf", [128, CH // 4 * L], "a")
        zeros = place("zeros", [L, D], "su")
        Wp = place("Wp", [128, KT, D], "a")
        wout = place("wout", [D, D], "a")
        wce = place("wce", [D, D], "a")
        assert end["a"] <= end["w"] + SA, (end["a"] - end["w"], SA)
        w1h = place("w1h", [D, NX, F], "w", F32R)
        w1l = place("w1l", [D, NX, F], "w", F32R)
        w2h = place("w2h", [128, NX, FO, D], "w", F32R)
        w2l = place("w2l", [128, NX, FO, D], "w", F32R)
        Tt = place("Tt", [PAIR, HB, PAIR, D // HB], "b")
        yh = place("yh", [D, T], "y", F32R)
        yl = place("yl", [D, T], "y", F32R)
        cwb = place("cwb", [128, E, GT], "cw")
        yt = place("yt", [PAIR, GP, D], "gt")
        y32 = place("y32", [D, GT], "gt")
        lg = place("lg", [PAIR, GP, E], "gt")
        pr = place("pr", [PAIR, GP, E], "gt")
        eq = place("eq", [PAIR, GP, E], "gt")
        rank = place("rank", [PAIR, GP, E], "gt")
        hot = [place(f"hot{i}", [PAIR, GP, E], "gt") for i in range(2)]
        cw = place("cw", [PAIR, GP, E], "gt")
        red = place("red", [PAIR, GP], "gt")
        cwT = place("cwT", [GP * E, PAIR], "gt")
        assert end["gt"] <= end["b"], (end["gt"], end["b"])
        Vr = place("Vr", [128, HP, KIND], "b1")
        Vq = place("Vq", [128, HP, KIND], "b1")
        VR = place("VR", [128, CH, 2 * KIND], "b1")
        VQ = place("VQ", [128, CH, 2 * KIND], "b1")
        bT = place("bT", [128, CH, L], "b1")
        dT = place("dT", [128, CH, L], "b1")
        end["kt"] = end["b1"]
        kt = place("kt", [L, 12, D], "kt")
        RT = place("RT", [128, CH, L], "b1")
        QT = place("QT", [128, CH, L], "b1")
        prod = place("prod", [128, 14, HP], "su")
        par = place("par", [128, 8, HP], "b1")
        skip = place("skip", [L, D], "b1")
        assert end["b1"] <= end["b"] - SB_ // 2, (end["b1"], end["b"])
        raw1 = place("raw1", [128, NX * FO, D], "st")
        raw2 = place("raw2", [D, NX, F], "st")
        cv = [place(f"cv{i}", [128, 4 * PAIR], "cv") for i in range(2)]
        gf = [place(f"gf{i}", [128, FO, GT], "g") for i in range(2)]
        gh = [place(f"gh{i}", [128, FO, GT], "g", F32R) for i in range(2)]
        gl = [place(f"gl{i}", [128, FO, GT], "g", F32R) for i in range(2)]
        h = place("h", [PAIR, NPAIR, D], "h")
        u = place("u", [PAIR, NPAIR, D], "u")
        acc = place("acc", [D, GT], "o")
        tmp = [place(f"tmp{i}", [D, GT], "o") for i in range(2)]
        osb = place("osb", [PAIR, GP, D], "o")
        ident = place("ident", [128, 128], "k")
        wsp = place("wsp", [D, DS], "k")
        brow = place("brow", [1, 2, D], "su")
        bsp = place("bsp", [PAIR, DS], "k")
        gbb = place("gbb", [PAIR, E], "k")
        gwT = place("gwT", [D, E], "k")
        vcol = place("vcol", [D, NV], "k")
        posb = place("posb", [D, L], "k")
        sb2s = place("sb2s", [D, 1], "k")
        tan2 = place("tan2", [128, L], "k")
        tcol = place("tcol", [L, 1], "k")
        dft = place("dft", [L, 2 * L], "k")
        s2 = place("s2", [128, HP], "k")
        a1 = place("a1", [128, HP], "k")
        a2 = place("a2", [128, HP], "k")
        eps = place("eps", [PAIR, 2 * GP], "k")
        mhalf = place("mhalf", [PAIR, 2 * GP], "k")
        mv = [place(f"mv{i}", [PAIR, 2 * GP, 2], "k") for i in range(2)]
        st = [place(f"st{i}", [PAIR, 2 * GP, 6], "k") for i in range(2)]
        rstd = [place(f"rstd{i}", [PAIR, 2 * GP], "k") for i in range(2)]
        shift = place("shift", [PAIR, 2 * GP], "k")
        sp = place("sp", [PAIR, 2 * GP, DS], "k")
        k0 = place("k0", [PAIR, 2 * GP], "k")
        none = place("none", [PAIR, 2 * GP], "k")
        ones = place("ones", [1, PAIR], "k", F32R)
        bhi = place("bhi", [1, 2, D], "k", F32R)
        blo = place("blo", [1, 2, D], "k", F32R)
        ksb = place("ksb", [L, D], "k")
        rev = place("rev", [PAIR, E], "k")
        assert end["k"] <= nc.sbuf_usable_end, (end["k"], nc.sbuf_usable_end)
        kpad = nc.dram_tensor("kpad", [HB, 2 * L, D // HB], F32).ap()
        cwd = nc.dram_tensor("cwd", [NG, GP, E, PAIR], F32).ap()
        bank = [ctx.enter_context(nc.psum_tensor(f"bank{i}", [128, 512], F32)) for i in range(8)]

        ld_par, ld_tok, ld_vec, ld_wp = sem("ld_par"), sem("ld_tok"), sem("ld_vec"), sem("ld_wp")
        ld_x = [sem(f"ld_x{c}") for c in range(C)]
        ld_raw, ld_skip, ld_zero, ld_zero0 = sem("ld_raw"), sem("ld_skip"), sem("ld_zero"), sem("ld_zero0")
        ld_toep = [sem(f"ld_toep{i}") for i in range(HB)]
        ld_cw = [sem(f"ld_cw{e}") for e in range(E)]
        st_zero, st_k, st_cw, st_out = sem("st_zero"), sem("st_k"), sem("st_cw"), sem("st_out")
        lsrep_ready, par_T, ls_T, vec_T = sem("lsrep_ready"), sem("par_T"), sem("ls_T"), sem("vec_T")
        wcT_ready, wce_T, tok_const, s2_ready = sem("wcT_ready"), sem("wce_T"), sem("tok_const"), sem("s2_ready")
        zero_ready, coef_ready, pool_const = sem("zero_ready"), sem("coef_ready"), sem("pool_const")
        bias_ready = sem("bias_ready")
        b_ready, sq_ready, rec_ready, q_ready = (sem(n) for n in ("b_ready", "sq_ready", "rec_ready", "q_ready"))
        cauchy_done, kf_ready, kf_T, kk_ready, at_ready, k_T, k_ready = (sem(n) for n in (
            "cauchy_done", "kf_ready", "kf_T", "kk_ready", "at_ready", "k_T", "k_ready"))
        tp_done = [sem(f"tp_done{i}") for i in range(2)]
        tp_copied = [sem(f"tp_copied{i}") for i in range(2)]
        x_sorted = [sem(f"x_sorted{c}") for c in range(C)]
        proj_done, xT_ready, a_done, xtok_ready, xtok_used, xn_ready = (
            [sem(f"{n}{i}") for i in range(2)] for n in
            ("proj_done", "xT_ready", "a_done", "xtok_ready", "xtok_used", "xn_ready"))
        xnT_done, xnT_ready, wout_done, h_ready, u_ready = (
            [sem(f"{n}{i}") for i in range(2)] for n in
            ("xnT_done", "xnT_ready", "wout_done", "h_ready", "u_ready"))
        stats_ready, rstd_ready = ([sem(f"{n}{i}") for i in range(2)] for n in ("stats_ready", "rstd_ready"))
        w_T, w_hi, w_lo = sem("w_T"), sem("w_hi"), sem("w_lo")
        conv_done, conv_copied, conv_T, conv_read = sem("conv_done"), sem("conv_copied"), sem("conv_T"), sem("conv_read")
        stats2, rstd2, y_ready, y_T, yh_ready, yl_ready = (sem(n) for n in (
            "stats2", "rstd2", "y_ready", "y_T", "yh_ready", "yl_ready"))
        gate_done, lg_ready, exp_ready, cw_ready, cw_T, cwT_ready = (sem(n) for n in (
            "gate_done", "lg_ready", "exp_ready", "cw_ready", "cw_T", "cwT_ready"))
        up_done, act_done, split_done, down_done = sem("up_done"), sem("act_done"), sem("split_done"), sem("down_done")
        scaled, added, out_T, out_ready = sem("scaled"), sem("added"), sem("out_T"), sem("out_ready")

        block = ctx.enter_context(nc.Block())

        def weights(i, w1, w2):
            return w1[:, i, :] if i < NX else w2[:, i - NX, :, :].rearrange("p o d -> p (o d)")

        def rows(v):
            return v.unsqueeze(0)

        def over_l(v, k):
            return v[:, bass.ds(CH * k, CH)].unsqueeze(2).broadcast_to([128, CH, L])

        def cauchy_b(engine, ops, k):
            ops.tensor_tensor(bT[:, :, :], over_l(s2, k), tan2[:, :].unsqueeze(1).broadcast_to([128, CH, L]), ALU.mult)
            engine.drain()
            ops.tensor_tensor(bT[:, :, :], bT[:, :, :], over_l(par[:, 7, :], k), ALU.subtract).then_inc(b_ready, 1)

        def conv_weights(i):
            return W_CONV + i * (W_END - W_CONV) // CONVS

        def conv_channel(i):
            return (i * CONV_H + D // 2) % D

        def pairs(k, half):
            return bass.ds(2 * GP * k + GP * half, GP)

        @block.sync
        def _(sp_):
            def load_x(k, c):
                src = x[bass.ds(TI * k, TI), c].rearrange("b (p i) w -> b p (i w)", p=NH)
                sp_.dma_start(Xc[c][:, :], src).then_inc(ld_x[c], 16)

            def load(dst, src, s):
                sp_.dma_start(dst, src).then_inc(s, 16)

            for c in range(C):
                load_x(0, c)
                if c == 0:
                    load(lsraw[:, :], log_step.rearrange("(a b) -> a b", b=2), ld_par)
                    load(Wp[:, :, :], W_patch.rearrange("(t p) d -> p t d", p=128), ld_wp)
            load(tan2[:, :], c_tan[0:1, :].broadcast_to([128, L]), ld_tok)
            load(wsp[:, :], W_spinor, ld_tok)
            load(wout[:, :], W_out, ld_tok)
            load(brow[:, 0, :], rows(b_embed), ld_tok)
            load(brow[:, 1, :], rows(b_out), ld_tok)
            load(bsp[:, :], rows(b_spinor).broadcast_to([PAIR, DS]), ld_tok)
            load(tcol[:, :], c_tan[1, :].unsqueeze(1), ld_tok)
            load(dft[:, :], c_dft, ld_tok)
            load(gbb[:, :], rows(gate_b).broadcast_to([PAIR, E]), ld_tok)
            sp_.wait_ge(zero_ready, 1)
            sp_.dma_start(kpad[:, L:2 * L, :].rearrange("b l d -> l b d"),
                          zeros[:, :].rearrange("l (b d) -> l b d", b=HB)).then_inc(st_zero, 16)
            sp_.dma_start(skip[L - 1:L, :], D_.unsqueeze(0)).then_inc(ld_skip, 16)
            with sp_.Fori(1, TILES) as k:
                for c in range(C):
                    sp_.wait_ge(x_sorted[c], k)
                    load_x(k, c)
            sp_.wait_ge(bias_ready, 1)
            sp_.wait_ge(st_zero, 16)
            for dst, src in ((raw1[:, 0:NS * FO, :], sw1), (raw1[:, NS * FO:NX * FO, :], rw1)):
                sp_.dma_start(dst, src.rearrange("e (o p) d -> p (e o) d", p=128)).then_inc(ld_raw, 16)
            for dst, src in ((raw2[:, 0:NS, :], sw2), (raw2[:, NS:NX, :], rw2)):
                sp_.dma_start(dst, src.rearrange("e d f -> d e f")).then_inc(ld_raw, 16)
            sp_.wait_ge(st_zero, 16)

            def zero_block(b, lo, hi, s):
                src = kpad[lo:hi, L:2 * L, :].rearrange("b l h -> b (l h)").unsqueeze(0).broadcast_to([L, hi - lo, L * D // HB])
                dst = Tt[b * L:(b + 1) * L, lo:hi, b * L:(b + 1) * L, :].rearrange("m b l h -> m b (l h)")
                sp_.dma_start(dst, src).then_inc(s, 16)

            def toeplitz(block):
                for b in range(2):
                    src = bass.AP(kpad.tensor, block * 2 * L * (D // HB), [[D // HB, L], [1, L * D // HB]])
                    dst = Tt[b * L:(b + 1) * L, block, (1 - b) * L:(2 - b) * L, :].rearrange("m l h -> m (l h)")
                    sp_.dma_start(dst, src).then_inc(ld_toep[block], 16)

            zero_block(0, HALF, HB, ld_zero)
            sp_.wait_ge(cauchy_done, TILES)
            zero_block(1, 0, HB, ld_zero)
            sp_.wait_ge(k_ready, 1)
            sp_.dma_start(kpad[:, 0:L, :].rearrange("b l d -> l b d"),
                          ksb[:, :].rearrange("l (b d) -> l b d", b=HB)).then_inc(st_k, 16)
            sp_.wait_ge(st_k, 16)
            for block in range(HALF, HB):
                toeplitz(block)
            zero_block(0, 0, HALF, ld_zero0)
            for block in range(HALF):
                toeplitz(block)

            def routing(c, first):
                sp_.wait_ge(cwT_ready, c + 1)
                sp_.dma_start(cwd[bass.ds(c, 1)].rearrange("c g e t -> (c g e) t"), cwT[:, :]).then_inc(st_cw, 16)
                sp_.wait_ge(st_cw, 16 * (c + 1))
                for e in range(E):
                    if not first:
                        sp_.wait_ge(scaled, 9 * (c - 1) + e + 2)
                    src = cwd[bass.ds(c, 1), :, e, :].broadcast_to([128, GP, PAIR])
                    sp_.dma_start(cwb[:, e, :].rearrange("p (g t) -> p g t", g=GP), src).then_inc(ld_cw[e], 16)

            def store(c):
                sp_.wait_ge(out_ready, c + 1)
                dst = out.rearrange("b l d -> (b l) d")[bass.ds(GT * c, GT), :].rearrange("(p i) d -> i p d", p=GP)
                sp_.dma_start(dst, osb[:, :, :]).then_inc(st_out, 16)

            routing(0, True)
            with sp_.Fori(1, NG) as c:
                routing(c, False)
                store(c - 1)
            store(NG - 1)
            sp_.wait_ge(st_out, 16 * NG)

        @block.gpsimd
        def _(pool):
            def load(dst, src):
                pool.dma_start(dst, src).then_inc(ld_vec, 16)

            load(prow[:, :], pos_embed[0])
            for at, src in ((V_BPATCH, rows(b_patch)), (V_GAMMA, rows(ln_gamma)), (V_BETA, rows(ln_beta)), (V_RB2, rb2),
                            (V_SB2, sb2), (V_B1, sb1.rearrange("e (o p) -> (e o) p", p=128)),
                            (V_B1 + NS * FO, rb1.rearrange("e (o p) -> (e o) p", p=128))):
                load(vrows[at:at + src.shape[0], :], src)
            load(wcrow[:, :], W_coord)
            load(gwrow[:, :], gate_w)
            load(we[:, :], W_embed)
            load(bccol[:, :], b_coord.unsqueeze(1))
            nc.gpsimd.memset(skip[:, :], 0.0)
            nc.gpsimd.memset(zeros[:, :], 0.0).then_inc(zero_ready, 1)
            nc.gpsimd.memset(VR[:, :, :], 0.0)
            nc.gpsimd.memset(VQ[:, :, :], 0.0)
            for e in range(E):
                nc.gpsimd.memset(rev[:, e:e + 1], float(E - e))
            nc.gpsimd.memset(none[:, :], 0.0)
            nc.gpsimd.memset(eps[:, :], LN_EPS)
            nc.gpsimd.memset(mhalf[:, :], -0.5).then_inc(pool_const, 1)
            pool.wait_ge(pool_const, 1)

            def inv_std(i, n):
                nc.gpsimd.tensor_tensor(rstd[i][:, 0:n], mv[i][:, 0:n, 1], eps[:, 0:n], ALU.add)
                pool.drain()
                return nc.gpsimd.tensor_tensor(rstd[i][:, 0:n], rstd[i][:, 0:n], mhalf[:, 0:n], ALU.pow)

            def shifts(i, n):
                pool.drain()
                nc.gpsimd.tensor_tensor(shift[:, 0:n], mv[i][:, 0:n, 0], rstd[i][:, 0:n], ALU.mult)
                pool.drain()
                return nc.gpsimd.tensor_tensor(shift[:, 0:n], none[:, 0:n], shift[:, 0:n], ALU.subtract)

            for k in range(TILES + 1):
                if k < TILES:
                    if k == 0:
                        pool.wait_ge(coef_ready, 1)
                    else:
                        pool.wait_ge(cauchy_done, k)
                    for b in range(2):
                        part, cols, turn = slice(64 * b, 64 * b + 64), slice(KIND * b, KIND * (b + 1)), slice(CH * k, CH * (k + 1))
                        nc.gpsimd.tensor_copy(VR[part, :, cols], Vr[part, turn, :])
                        nc.gpsimd.tensor_copy(VQ[part, :, cols], Vq[part, turn, :])
                        pool.drain()
                    pool.wait_ge(rec_ready, k + 1)
                    nc.gpsimd.tensor_tensor(RT[:, :, :], dT[:, :, :], over_l(a1, k), ALU.mult)
                    nc.gpsimd.tensor_tensor(QT[:, :, :], dT[:, :, :], bT[:, :, :], ALU.mult).then_inc(q_ready, 1)
                if k >= 1:
                    pool.wait_ge(stats_ready[1], k)
                    inv_std(1, 2 * GP)
                    shifts(1, 2 * GP).then_inc(rstd_ready[1], 1)
                if k < TILES - 1:
                    pool.drain()
                    cauchy_b(pool, nc.gpsimd, k + 1)
                if k < TILES:
                    pool.wait_ge(stats_ready[0], k + 1)
                    inv_std(0, 2 * GP).then_inc(rstd_ready[0], 1)

            def second_norm(c, first):
                pool.wait_ge(stats2, c + 1)
                if not first:
                    pool.wait_ge(y_ready, c)
                inv_std(0, GP)
                shifts(0, GP).then_inc(rstd2, 1)

            def add_experts(c):
                for e in range(E):
                    pool.wait_ge(scaled, 9 * c + e + 2)
                    nc.gpsimd.tensor_tensor(acc[:, :], acc[:, :], tmp[e % 2][:, :], ALU.add).then_inc(added, 1)
                    pool.drain()

            second_norm(0, True)
            with pool.Fori(0, NG - 1) as c:
                second_norm(c + 1, False)
                add_experts(c)
            add_experts(NG - 1)

        @block.scalar
        def _(act):
            act.dma_start(ident[:, :], c_ident).then_inc(ld_par, 16)
            for dst, src in ((praw, P_), (braw, B_), (craw, C_)):
                act.dma_start(dst[:, :, :], src.rearrange("(a b) n t -> a (b n) t", b=2)).then_inc(ld_par, 16)
            for dst, src in ((lre, Lambda_re), (lim, Lambda_im)):
                act.dma_start(dst[:, :], src.rearrange("(a b) n -> a (b n)", b=2)).then_inc(ld_par, 16)

            def copy_patches(k, t):
                for i, (lo, hi) in enumerate(((0, 4), (4, NH))):
                    act.wait_ge(tp_done[i], KT * k + t + 1)
                    nc.scalar.copy(patchT[:, t, lo:hi, :].rearrange("p w r -> p (w r)"),
                                   bank[i][:, 0:(hi - lo) * TR]).then_inc(tp_copied[i], 1)

            def keep_sums(k):
                act.wait_ge(kf_T, k + 1)
                nc.scalar.copy(kk[:, bass.ds(2 * CH * k, 2 * CH), :].rearrange("p (c two) v -> p c (two v)", two=2),
                               bank[3][0:L, :].rearrange("p (c v) -> p c v", v=32)[:, :, 0:2 * KIND]).then_inc(kk_ready, 1)

            def sort_pixels(k, c):
                act.wait_ge(ld_x[c], 16 * (k + 1))
                nc.scalar.copy(Xr[c][:, :, :, :].rearrange("r w i j -> r i w j"),
                               Xc[c][:, :].rearrange("r (i w j) -> r i w j", i=P, w=NH)).then_inc(x_sorted[c], 1)

            def back(k, half):
                act.wait_ge(xnT_done[half], k + 1)
                nc.scalar.activation(xnT[half][:, :], bank[7 - half][:, 0:GT], ACT.Identity, scale=vcol[:, V_GAMMA:V_GAMMA + 1],
                                     bias=vcol[:, V_BETA:V_BETA + 1]).then_inc(xnT_ready[half], 1)

            def back_out(k, half):
                act.wait_ge(wout_done[half], k + 1)
                nc.scalar.copy(h[:, pairs(k, half), :].rearrange("p g d -> p (g d)"), bank[4 + half][0:PAIR, :]).then_inc(h_ready[half], 1)

            def conv_input(k, half):
                act.wait_ge(rstd_ready[1], k + 1)
                for g in range(GP):
                    n = GP * half + g
                    last = nc.scalar.activation(u[:, 2 * GP * k + n, :], h[:, 2 * GP * k + n, :], ACT.Identity,
                                                scale=rstd[1][:, n:n + 1], bias=shift[:, n:n + 1])
                last.then_inc(u_ready[half], 1)

            def tile(k, first, more):
                for t in range(KT):
                    copy_patches(k, t)
                    if t == 0 and not first:
                        keep_sums(k - 1)
                    if t == (1 if first else 2):
                        act.wait_ge(b_ready, k + 1)
                        nc.scalar.activation(dT[:, :, :], bT[:, :, :], ACT.Square).then_inc(sq_ready, 1)
                    if t in (3, 4) and not first:
                        back(k - 1, t - 3)
                    if t == KT - 1 and not first:
                        for half in range(2):
                            back_out(k - 1, half)
                    if t % 2 == 1 and more:
                        sort_pixels(k + 1, t // 2)
                for half in range(2):
                    act.wait_ge(a_done[half], k + 1)
                    nc.scalar.copy(xtok[half][:, :, :].rearrange("p g d -> p (g d)"), bank[6 - 4 * half][0:PAIR, :]).then_inc(xtok_ready[half], 1)
                    if not first and half == 0:
                        conv_input(k - 1, half)
                act.wait_ge(cauchy_done, k + 1)
                if not first:
                    act.wait_ge(kf_T, k)
                nc.scalar.copy(kf[:, :], bank[3][:, 0:CH // 4 * L]).then_inc(kf_ready, 1)
                if not first:
                    conv_input(k - 1, 1)

            for c in range(C):
                sort_pixels(0, c)
            act.wait_ge(ls_T, 1)
            nc.scalar.activation(s2[:, :], bank[4][:, 0:HP], ACT.Exp, scale=-1.0).then_inc(s2_ready, 1)
            tile(0, True, True)
            with act.Fori(1, TILES - 1) as k:
                tile(k, False, True)
            tile(TILES - 1, False, False)

            def high_weights(lo, hi):
                for i in range(lo, hi):
                    act.wait_ge(w_T, i + 1)
                    nc.scalar.copy(weights(i, w1h, w2h), bank[i % 3][:, :]).then_inc(w_hi, 1)

            keep_sums(TILES - 1)
            high_weights(0, W_OUT)
            for half in range(2):
                back(TILES - 1, half)
            for half in range(2):
                back_out(TILES - 1, half)
            act.wait_ge(k_T, 1)
            nc.scalar.copy(ksb[:, :], bank[3][0:L, 384:512]).then_inc(k_ready, 1)
            high_weights(W_OUT, W_OUT + 2)
            conv_input(TILES - 1, 0)
            high_weights(W_OUT + 2, W_CONV)
            act.wait_ge(u_ready[0], TILES)
            act.wait_ge(u_ready[1], TILES)
            for i in range(CONVS):
                act.wait_ge(conv_done, i + 1)
                if i >= 2:
                    act.wait_ge(conv_T, i - 1)
                nc.scalar.copy(cv[i % 2][:, :].rearrange("p (s t) -> p s t", s=4),
                               bank[3 + 4 * (i % 2)][:, 0:4 * PAIR].rearrange("p (s t) -> p s t", s=4)[:, :, ::-1]).then_inc(conv_copied, 1)
                high_weights(conv_weights(i), conv_weights(i + 1))

            def norm(c, first):
                act.wait_ge(rstd2, c + 1)
                for g in range(GP):
                    last = nc.scalar.activation(yt[:, g, :], h[:, GP * c + g, :], ACT.Identity,
                                                scale=rstd[0][:, g:g + 1], bias=shift[:, g:g + 1])
                last.then_inc(y_ready, 1)

            def high_y(c, first):
                act.wait_ge(y_T, c + 1)
                if not first:
                    act.wait_ge(gate_done, c)
                    act.wait_ge(yl_ready, c)
                nc.scalar.copy(y32[:, :], bank[7][:, 0:GT])
                nc.scalar.copy(yh[:, bass.ds(GT * c, GT)], bank[7][:, 0:GT]).then_inc(yh_ready, 1)

            def exps(c):
                act.wait_ge(lg_ready, c + 1)
                nc.scalar.activation(pr[:, :, :], lg[:, :, :], ACT.Exp).then_inc(exp_ready, 1)

            def chunk(c, first, last):
                for e in range(NX):
                    if e == 3 and not last:
                        norm(c + 1, False)
                    if e == 5 and not last:
                        high_y(c + 1, False)
                    if e == 7 and not last:
                        exps(c + 1)
                    for o in range(FO):
                        act.wait_ge(up_done, FO * NX * c + FO * e + o + 1)
                        if o == 0 and not (first and e < 2):
                            act.wait_ge(split_done, 2 * (NX * c + e - 1))
                        b1 = vcol[:, V_B1 + FO * e + o:V_B1 + FO * e + o + 1]
                        gelu = nc.scalar.activation(gf[e % 2][:, o, :], bank[o][:, 0:GT], ACT.Gelu, bias=b1)
                        if o == FO - 1:
                            gelu = nc.scalar.activation(gh[e % 2][:, o, :], bank[o][:, 0:GT], ACT.Gelu, bias=b1)
                        gelu.then_inc(act_done, 1)

            high_weights(W_END, 2 * NX)
            norm(0, True)
            high_y(0, True)
            exps(0)
            chunk(0, True, False)
            with act.Fori(1, NG - 1) as c:
                chunk(c, False, False)
            chunk(NG - 1, False, True)

        @block.vector
        def _(dve):
            V = nc.vector
            dve.wait_ge(ld_par, 16 * 7)
            V.tensor_copy(lsrep[:, :, :], lsraw[:, :].unsqueeze(2).broadcast_to([HP, 2, N])).then_inc(lsrep_ready, 1)
            dve.wait_ge(par_T, 1)
            V.tensor_copy(par[:, :, :].rearrange("p a b -> p (a b)"), bank[7][:, :])
            dve.drain()
            Pr, Pi, Br, Bi, Cr, Ci, Lr, Li = (par[:, i, :] for i in range(8))
            V.tensor_scalar(a1[:, :], Lr, -1.0, 1e-4, ALU.mult, ALU.max)
            dve.drain()
            V.tensor_tensor(a2[:, :], a1[:, :], a1[:, :], ALU.mult)

            def cauchy_r(k):
                dve.wait_ge(sq_ready, k + 1)
                V.tensor_tensor(dT[:, :, :], dT[:, :, :], over_l(a2, k), ALU.add)
                dve.drain()
                V.reciprocal(dT[:, :, :], dT[:, :, :]).then_inc(rec_ready, 1)

            def token_stats(i, at, src):
                for g in range(GP):
                    V.bn_stats(st[i][:, at + g, :], src(g))
                dve.drain()
                for g in range(GP):
                    last = V.bn_aggr(mv[i][:, at + g, :], st[i][:, at + g, :])
                return last

            def evacuate_x(k, half, first):
                dve.wait_ge(proj_done[half], k + 1)
                if not first:
                    dve.wait_ge(a_done[half], k)
                V.tensor_tensor(xT[half][:, :].rearrange("p (b h w) -> p b h w", b=HR // NH, h=NH),
                                bank[2 + half][:, 0:GT].rearrange("p (w b h) -> p b h w", w=NH, h=NH),
                                posb[:, :].rearrange("p (h w) -> p h w", h=NH).unsqueeze(1).broadcast_to([D, HR // NH, NH, NH]),
                                ALU.add).then_inc(xT_ready[half], 1)

            def spinors(k):
                dve.wait_ge(a_done[1], k + 1)
                V.tensor_tensor(sp[:, :, :], bank[7][0:PAIR, GT:GT + 2 * GP * DS].rearrange("p (g s) -> p g s", s=DS),
                                bsp[:, :].unsqueeze(1).broadcast_to([PAIR, 2 * GP, DS]), ALU.add)
                dve.drain()
                V.tensor_tensor(sp[:, :, :], sp[:, :, :], sp[:, :, :], ALU.mult)
                dve.drain()
                V.tensor_reduce(k0[:, :], sp[:, :, :], AX.X, ALU.add)
                dve.drain()

            def enhance(k, half):
                dve.wait_ge(xtok_ready[half], k + 1)
                for g in range(GP):
                    last = V.scalar_tensor_tensor(xe[half][:, g, :], bank[4 + half][0:PAIR, g * D:(g + 1) * D],
                                                  k0[:, GP * half + g:GP * half + g + 1], xtok[half][:, g, :], ALU.mult, ALU.add)
                last.then_inc(xtok_used[half], 1)
                dve.drain()
                last = token_stats(0, GP * half, lambda g: xe[half][:, g, :])
                if half == 1:
                    last.then_inc(stats_ready[0], 1)

            def first_norm(k):
                dve.wait_ge(rstd_ready[0], k + 1)
                for half in range(2):
                    for g in range(GP):
                        n = GP * half + g
                        last = V.tensor_scalar(xe[half][:, g, :], xe[half][:, g, :], mv[0][:, n, 0:1], rstd[0][:, n:n + 1],
                                               ALU.subtract, ALU.mult)
                    last.then_inc(xn_ready[half], 1)

            def output_stats(k, half):
                dve.wait_ge(h_ready[half], k + 1)
                last = token_stats(1, GP * half, lambda g: h[:, 2 * GP * k + GP * half + g, :])
                if half == 1:
                    last.then_inc(stats_ready[1], 1)

            r00, i00, r01, i01, r10, i10, r11, i11 = (kk[:, :, i] for i in range(KIND))
            t = [kt[:, i, :] for i in range(12)]

            def tt(o, a, b, op):
                V.tensor_tensor(t[o], a, b, op)

            def root_products():
                dve.wait_ge(kk_ready, TILES)
                tt(0, r01, r10, ALU.mult); tt(1, i01, i10, ALU.mult); tt(2, r01, i10, ALU.mult); tt(3, i01, r10, ALU.mult)
                V.tensor_scalar(t[4], r11, 1.0, None, ALU.add); tt(5, i11, i11, ALU.mult)
                dve.drain()
                tt(6, t[0], t[1], ALU.subtract); tt(7, t[2], t[3], ALU.add); tt(8, t[4], t[4], ALU.mult)
                dve.drain()

            def at_roots():
                tt(8, t[8], t[5], ALU.add); tt(0, t[6], t[4], ALU.mult); tt(1, t[7], i11, ALU.mult)
                tt(2, t[7], t[4], ALU.mult); tt(3, t[6], i11, ALU.mult)
                dve.drain()
                V.reciprocal(t[8], t[8]); tt(0, t[0], t[1], ALU.add); tt(2, t[2], t[3], ALU.subtract)
                dve.drain()
                tt(0, t[0], t[8], ALU.mult); tt(2, t[2], t[8], ALU.mult)
                dve.drain()
                tt(0, r00, t[0], ALU.subtract); tt(2, i00, t[2], ALU.subtract)
                dve.drain()
                V.tensor_scalar(t[1], t[2], tcol[:, 0:1], None, ALU.mult); V.tensor_scalar(t[3], t[0], tcol[:, 0:1], None, ALU.mult)
                dve.drain()
                tt(10, t[0], t[1], ALU.subtract)
                V.tensor_tensor(t[11], t[2], t[3], ALU.add).then_inc(at_ready, 1)

            def low_weights(lo, hi):
                for i in range(lo, hi):
                    dve.wait_ge(w_hi, i + 1)
                    V.tensor_tensor(weights(i, w1l, w2l), bank[i % 3][:, :], weights(i, w1h, w2h).bitcast(F32),
                                    ALU.subtract).then_inc(w_lo, 1)

            def tile(k, first, more):
                if not first:
                    first_norm(k - 1)
                    cauchy_r(k)
                    output_stats(k - 1, 0)
                for half in range(2):
                    evacuate_x(k, half, first)
                if not first:
                    output_stats(k - 1, 1)
                spinors(k)
                for half in range(2):
                    enhance(k, half)
                if not more:
                    root_products()
                    first_norm(k)
                    at_roots()
                    low_weights(0, 1)
                dve.drain()

            dve.wait_ge(s2_ready, 1)
            dve.wait_ge(ld_tok, 16 * 9)
            dve.drain()
            cauchy_b(dve, V, 0)
            products = [(Cr, Br), (Ci, Bi), (Cr, Bi), (Ci, Br), (Cr, Pr), (Ci, Pi), (Cr, Pi), (Ci, Pr),
                        (Pr, Br), (Pi, Bi), (Pr, Bi), (Pi, Br), (Pr, Pr), (Pi, Pi)]
            for i, (p, q) in enumerate(products):
                V.tensor_tensor(prod[:, i, :], p, q, ALU.mult)
            V.memset(Vr[:, :, KIND - 1], 0.0)
            dve.drain()
            for i in range(7):
                V.tensor_tensor(Vr[:, :, i], prod[:, 2 * i, :], prod[:, 2 * i + 1, :], ALU.subtract if i in (1, 3, 5) else ALU.add)
            dve.drain()
            cauchy_r(0)
            V.tensor_copy(Vq[:, :, 0:KIND:2], Vr[:, :, 1:KIND:2])
            V.tensor_scalar(Vq[:, :, 1:KIND:2], Vr[:, :, 0:KIND:2], -1.0, None, ALU.mult).then_inc(coef_ready, 1)
            dve.wait_ge(vec_T, 1)
            dve.wait_ge(ld_vec, 16 * 12)
            V.tensor_copy(vcol[:, :], bank[5][:, 0:NV])
            V.tensor_copy(wcT[:, :], bank[5][0:DC, 128:256])
            V.tensor_copy(gwT[:, :], bank[5][:, 256:256 + E]).then_inc(wcT_ready, 1)
            dve.drain()
            V.tensor_scalar(posb[:, :], bank[5][:, 64:64 + L], vcol[:, V_BPATCH:V_BPATCH + 1], None, ALU.add)
            V.tensor_tensor(sb2s[:, :], vcol[:, V_SB2:V_SB2 + 1], vcol[:, V_SB2 + 1:V_SB2 + 2], ALU.add)
            dve.wait_ge(wce_T, 1)
            V.tensor_copy(wce[:, :], bank[6][:, 0:D])
            V.memset(ones[:, :].bitcast(F32), 1.0)
            V.tensor_tensor(brow[:, 0, :], brow[:, 0, :], bank[6][0:1, D:2 * D], ALU.add).then_inc(tok_const, 1)
            dve.drain()
            V.tensor_copy(bhi[:, :, :], brow[:, :, :])
            dve.drain()
            V.tensor_tensor(blo[:, :, :], brow[:, :, :], bhi[:, :, :].bitcast(F32), ALU.subtract).then_inc(bias_ready, 1)
            dve.wait_ge(pool_const, 1)
            dve.drain()
            tile(0, True, True)
            with dve.Fori(1, TILES - 1) as k:
                tile(k, False, True)
            tile(TILES - 1, False, False)

            for half in range(2):
                output_stats(TILES - 1, half)
            low_weights(1, 4)
            dve.wait_ge(rstd_ready[1], TILES)
            for g in range(GP):
                n = GP + g
                p = 2 * GP * (TILES - 1) + n
                last = V.tensor_scalar(u[:, p, :], h[:, p, :], mv[1][:, n, 0:1], rstd[1][:, n:n + 1], ALU.subtract, ALU.mult)
            last.then_inc(u_ready[1], 1)
            low_weights(4, W_CONV)
            for i in range(CONVS):
                low_weights(conv_weights(i), conv_weights(i + 1))
                dve.wait_ge(conv_T, i + 1)
                part = h[:, :, conv_channel(i):conv_channel(i) + CONV_H]
                V.tensor_tensor(part, part, bank[4 + i % 3][0:PAIR, :].rearrange("p (c g) -> p g c", c=CONV_H),
                                ALU.add).then_inc(conv_read, 1)
            dve.drain()

            def second_stats(c, first):
                if not first:
                    dve.wait_ge(y_ready, c)
                token_stats(0, 0, lambda g: h[:, GP * c + g, :]).then_inc(stats2, 1)

            def low_y(c):
                dve.wait_ge(yh_ready, c + 1)
                span = bass.ds(GT * c, GT)
                V.tensor_tensor(yl[:, span], y32[:, :], yh[:, span].bitcast(F32), ALU.subtract).then_inc(yl_ready, 1)

            def split(c, e, first):
                for p in range(2):
                    dve.wait_ge(act_done, FO * NX * c + FO * e + 2 * p + 2)
                    if p == 0 and not (first and e < 2):
                        dve.wait_ge(down_done, NX * c + e - 1)
                    span = slice(2 * p, 2 * p + 2)
                    own = slice(2 * p, 2 * p + 2 - p)
                    V.tensor_copy(gh[e % 2][:, own, :], gf[e % 2][:, own, :])
                    dve.drain()
                    V.tensor_tensor(gl[e % 2][:, span, :], gf[e % 2][:, span, :], gh[e % 2][:, span, :].bitcast(F32),
                                    ALU.subtract).then_inc(split_done, 1)

            def wide(v):
                return v[:, :].unsqueeze(2).broadcast_to([PAIR, GP, E])

            def gate_logits(c):
                dve.wait_ge(gate_done, c + 1)
                V.tensor_tensor(lg[:, :, :], bank[7][0:PAIR, 0:GP * E].rearrange("p (g e) -> p g e", e=E),
                                gbb[:, :].unsqueeze(1).broadcast_to([PAIR, GP, E]), ALU.add)
                dve.drain()
                V.tensor_reduce(red[:, :], lg[:, :, :], AX.X, ALU.max)
                dve.drain()
                V.tensor_tensor(lg[:, :, :], lg[:, :, :], wide(red), ALU.subtract).then_inc(lg_ready, 1)

            def rank_highest(src):
                V.tensor_reduce(red[:, :], src[:, :, :], AX.X, ALU.max)
                dve.drain()
                V.tensor_tensor(eq[:, :, :], src[:, :, :], wide(red), ALU.is_equal)
                dve.drain()
                V.tensor_tensor(rank[:, :, :], eq[:, :, :], rev[:, :].unsqueeze(1).broadcast_to([PAIR, GP, E]), ALU.mult)
                dve.drain()

            def pick_first(n):
                V.tensor_reduce(red[:, :], rank[:, :, :], AX.X, ALU.max)
                dve.drain()
                V.tensor_tensor(hot[n][:, :, :], rank[:, :, :], wide(red), ALU.is_equal)
                dve.drain()

            def gate_probs(c):
                dve.wait_ge(exp_ready, c + 1)
                V.tensor_reduce(red[:, :], pr[:, :, :], AX.X, ALU.add)
                dve.drain()
                V.reciprocal(red[:, :], red[:, :])
                dve.drain()
                V.tensor_tensor(pr[:, :, :], pr[:, :, :], wide(red), ALU.mult)
                dve.drain()
                rank_highest(pr)

            def gate_second():
                pick_first(0)
                V.scalar_tensor_tensor(lg[:, :, :], hot[0][:, :, :], -2.0, pr[:, :, :], ALU.mult, ALU.add)
                dve.drain()
                rank_highest(lg)

            def gate_weights():
                pick_first(1)
                V.tensor_tensor(eq[:, :, :], hot[0][:, :, :], hot[1][:, :, :], ALU.add)
                dve.drain()
                V.tensor_tensor(cw[:, :, :], eq[:, :, :], pr[:, :, :], ALU.mult).then_inc(cw_ready, 1)

            def gate_rows(c, first):
                dve.wait_ge(cw_T, c + 1)
                if not first:
                    dve.wait_ge(st_cw, 16 * c)
                V.tensor_copy(cwT[:, :], bank[7][0:GP * E, 0:PAIR]).then_inc(cwT_ready, 1)

            def combine(c, unit, first):
                src = bank[4 + unit % 3][:, 0:GT]
                dve.wait_ge(down_done, NX * c + unit + 2)
                if unit == 0:
                    if not first:
                        dve.wait_ge(out_T, c)
                    V.tensor_scalar(acc[:, :], src, sb2s[:, 0:1], None, ALU.add).then_inc(scaled, 1)
                    return
                e = unit - 1
                dve.wait_ge(ld_cw[e], 16 * (c + 1))
                if not (first and e < 2):
                    dve.wait_ge(added, E * c + e - 1)
                V.scalar_tensor_tensor(tmp[e % 2][:, :], src, vcol[:, V_RB2 + e:V_RB2 + e + 1], cwb[:, e, :],
                                       ALU.add, ALU.mult).then_inc(scaled, 1)

            def output(c, first):
                dve.wait_ge(out_T, c + 1)
                if not first:
                    dve.wait_ge(st_out, 16 * c)
                V.tensor_tensor(osb[:, :, :], bank[7][0:PAIR, :].rearrange("p (g d) -> p g d", g=GP),
                                h[:, bass.ds(GP * c, GP), :], ALU.add).then_inc(out_ready, 1)

            def chunk(c, first, second, last):
                for e in range(NX):
                    split(c, e, first)
                    if e == 0 and not first:
                        combine(c - 1, NX - 2, second)
                    if e == 2 and not first:
                        output(c - 1, second)
                    if first:
                        if e == 0:
                            gate_probs(0)
                        if e == 1:
                            gate_second()
                        if e == 2:
                            gate_weights()
                            combine(0, 0, True)
                        if e == 3:
                            gate_rows(0, True)
                        if e >= 4:
                            combine(0, e - 3, True)
                        if e == NX - 1:
                            combine(0, NX - 3, True)
                    elif e >= 2:
                        combine(c, e - 2, False)
                    if not last:
                        if e == 0:
                            second_stats(c + 1, False)
                        if e == 4:
                            low_y(c + 1)
                        if e == 5:
                            gate_logits(c + 1)
                        if e == 6:
                            gate_probs(c + 1)
                        if e == 7:
                            gate_second()
                        if e == 8:
                            gate_weights()
                        if e == 9:
                            gate_rows(c + 1, False)

            second_stats(0, True)
            low_weights(W_END, 2 * NX)
            low_y(0)
            gate_logits(0)
            chunk(0, True, False, False)
            chunk(1, False, True, False)
            with dve.Fori(2, NG - 1) as c:
                chunk(c, False, False, False)
            chunk(NG - 1, False, False, True)
            combine(NG - 1, NX - 2, False)
            output(NG - 1, False)

        @block.tensor
        def _(pe):
            MM, TP = nc.tensor.matmul, nc.tensor.transpose

            def to_columns(dst, src):
                rows_ = src.shape[0]
                return TP(dst, src, ident[0:rows_, 0:rows_])

            pe.wait_ge(ld_par, 16 * 7)
            for i, src in enumerate((praw[:, :, 0], praw[:, :, 1], braw[:, :, 0], braw[:, :, 1], craw[:, :, 0], craw[:, :, 1],
                                     lre[:, :], lim[:, :])):
                last = to_columns(bank[7][:, i * HP:(i + 1) * HP], src)
            last.then_inc(par_T, 1)
            pe.wait_ge(lsrep_ready, 1)
            to_columns(bank[4][:, 0:HP], lsrep[:, :, :].rearrange("p b n -> p (b n)")).then_inc(ls_T, 1)
            def transpose_patches(k, t, first):
                c, top = t // 2, t % 2
                if top == 0:
                    pe.wait_ge(x_sorted[c], k + 1)
                src = Xr[c][:, :, top * 8:top * 8 + 8, :].rearrange("r w i j -> r w (i j)")
                for i, (lo, hi) in enumerate(((0, 4), (4, NH))):
                    if not (first and t == 0):
                        pe.wait_ge(tp_copied[i], KT * k + t)
                    if t == 0 and i == 1 and not first:
                        pe.wait_ge(kf_ready, k)
                    for w in range(lo, hi):
                        last = to_columns(bank[i][:, (w - lo) * TR:(w - lo + 1) * TR], src[:, w, :])
                    last.then_inc(tp_done[i], 1)

            def project(k, t, first):
                for i in range(2):
                    pe.wait_ge(tp_copied[i], KT * k + t + 1)
                if t == 0 and not first:
                    pe.wait_ge(xtok_ready[1], k)
                    pe.wait_ge(kk_ready, k)
                for half in range(2):
                    last = MM(bank[2 + half][:, 0:GT], Wp[:, t, :], patchT[:, t, :, half * HR:(half + 1) * HR],
                              start=t == 0, stop=t == KT - 1)
                    if t == KT - 1:
                        last.then_inc(proj_done[half], 1)

            def add_bias(dst, i):
                for n, part in enumerate((bhi, blo)):
                    MM(dst[0:PAIR, :], ones[:, :], part[:, i, :].unsqueeze(1).broadcast_to([1, GP, D]), start=n == 0, stop=False)

            def embed(k, half, first):
                pe.wait_ge(xT_ready[half], k + 1)
                if not first:
                    pe.wait_ge(h_ready[half], k)
                    pe.wait_ge(xnT_ready[half], k)
                add_bias(bank[4 + half], 0)
                for g in range(GP):
                    tok = xT[half][:, g * PAIR:(g + 1) * PAIR]
                    MM(bank[4 + half][0:PAIR, g * D:(g + 1) * D], tok, wce[:, :], start=False, stop=g == GP - 1)
                    at = GT + DS * (GP * half + g)
                    MM(bank[7][0:PAIR, at:at + DS], tok, wsp[:, :], start=True, stop=True)
                    last = TP(bank[6 - 4 * half][0:PAIR, g * D:(g + 1) * D], tok, ident[:, :])
                last.then_inc(a_done[half], 1)

            def cauchy(k):
                pe.wait_ge(q_ready, k + 1)
                for i in range(CH):
                    group, quarter = i // 4, i % 4
                    dst = bank[3][32 * quarter:32 * quarter + 2 * KIND, group * L:(group + 1) * L]
                    MM(dst, VR[:, i, :], RT[:, i, :], start=True, stop=False, tile_position=(0, 32 * quarter))
                    last = MM(dst, VQ[:, i, :], QT[:, i, :], start=False, stop=True, tile_position=(0, 32 * quarter))
                last.then_inc(cauchy_done, 1)

            def transpose_sums(k):
                for group in range(CH // 4):
                    last = to_columns(bank[3][0:L, group * 128:(group + 1) * 128], kf[:, group * L:(group + 1) * L])
                last.then_inc(kf_T, 1)

            def transpose_norm(k, half):
                pe.wait_ge(xn_ready[half], k + 1)
                if half == 1:
                    pe.wait_ge(xtok_ready[0], k + 1)
                for g in range(GP):
                    last = to_columns(bank[7 - half][:, g * PAIR:(g + 1) * PAIR], xe[half][:, g, :])
                last.then_inc(xnT_done[half], 1)

            def project_out(k, half):
                pe.wait_ge(xnT_ready[half], k + 1)
                pe.wait_ge(xtok_used[half], k + 1)
                add_bias(bank[4 + half], 1)
                for g in range(GP):
                    last = MM(bank[4 + half][0:PAIR, g * D:(g + 1) * D], xnT[half][:, g * PAIR:(g + 1) * PAIR], wout[:, :],
                              start=False, stop=g == GP - 1)
                last.then_inc(wout_done[half], 1)

            def tile(k, first):
                for t in range(KT):
                    transpose_patches(k, t, first)
                    if t == 0 and first:
                        pe.wait_ge(ld_wp, 16)
                    if t == 0 and not first:
                        transpose_sums(k - 1)
                    if t >= 1:
                        project(k, t - 1, first)
                    if t == 3 and first:
                        pe.wait_ge(ld_vec, 16 * 12)
                        to_columns(bank[5][:, 0:NV], vrows[:, :])
                        to_columns(bank[5][:, 64:64 + L], prow[:, :])
                        to_columns(bank[5][0:DC, 128:256], wcrow[:, :])
                        to_columns(bank[5][:, 256:256 + E], gwrow[:, :]).then_inc(vec_T, 1)
                    if t in (3, 4) and not first:
                        transpose_norm(k - 1, t - 3)
                    if t == KT - 1 and not first:
                        project_out(k - 1, 0)
                project(k, KT - 1, first)
                if not first:
                    project_out(k - 1, 1)
                if first:
                    pe.wait_ge(wcT_ready, 1)
                    MM(bank[6][:, 0:D], wcT[:, :], we[:, :], start=True, stop=True)
                    MM(bank[6][0:1, D:2 * D], bccol[:, :], we[:, :], start=True, stop=True).then_inc(wce_T, 1)
                    pe.wait_ge(tok_const, 1)
                    pe.wait_ge(bias_ready, 1)
                for half in range(2):
                    embed(k, half, first)
                cauchy(k)

            tile(0, True)
            with pe.Fori(1, TILES) as k:
                tile(k, False)

            def transpose_weights(lo, hi):
                for i in range(lo, hi):
                    if i >= 3:
                        pe.wait_ge(w_lo, i - 2)
                    for o in range(FO):
                        src = raw1[:, i * FO + o, :] if i < NX else raw2[:, i - NX, o * 128:(o + 1) * 128]
                        last = to_columns(bank[i % 3][:, o * 128:(o + 1) * 128], src)
                    last.then_inc(w_T, 1)

            def convolve(i):
                block, at = divmod(conv_channel(i), D // HB)
                if at == 0:
                    pe.wait_ge(ld_toep[block], 32)
                if i == CONVS // 2:
                    pe.wait_ge(ld_zero0, 16)
                if i >= 2:
                    pe.wait_ge(conv_copied, i - 1)
                for c in range(CONV_H):
                    slot, quarter = c // 4, c % 4
                    last = MM(bank[3 + 4 * (i % 2)][quarter * NPAIR:(quarter + 1) * NPAIR, slot * PAIR:(slot + 1) * PAIR],
                              u[:, :, conv_channel(i) + c], Tt[:, block, :, at + c], start=True, stop=True,
                              tile_position=(0, quarter * NPAIR))
                last.then_inc(conv_done, 1)

            def transpose_conv(i):
                pe.wait_ge(conv_copied, i + 1)
                if i >= 3:
                    pe.wait_ge(conv_read, i - 2)
                for slot in range(4):
                    last = to_columns(bank[4 + i % 3][0:PAIR, slot * 128:(slot + 1) * 128], cv[i % 2][:, slot * PAIR:(slot + 1) * PAIR])
                last.then_inc(conv_T, 1)

            pe.wait_ge(kf_ready, TILES)
            transpose_sums(TILES - 1)
            pe.wait_ge(ld_raw, 64)
            pe.wait_ge(xtok_ready[1], TILES)
            transpose_weights(0, W_OUT)
            for half in range(2):
                transpose_norm(TILES - 1, half)
            for half in range(2):
                project_out(TILES - 1, half)
            pe.wait_ge(ld_skip, 16)
            pe.wait_ge(at_ready, 1)
            MM(bank[3][0:L, 384:512], dft[:, 0:L], kt[:, 10, :], start=True, stop=False)
            MM(bank[3][0:L, 384:512], dft[:, L:2 * L], kt[:, 11, :], start=False, stop=False)
            MM(bank[3][0:L, 384:512], ident[0:L, 0:L], skip[:, :], start=False, stop=True).then_inc(k_T, 1)
            transpose_weights(W_OUT, W_CONV)
            pe.wait_ge(ld_zero, 32)
            for half in range(2):
                pe.wait_ge(u_ready[half], TILES)
                pe.wait_ge(h_ready[half], TILES)
                pe.wait_ge(xnT_ready[half], TILES)
            for i in range(CONVS):
                convolve(i)
                transpose_weights(conv_weights(i), conv_weights(i + 1))
                if i >= 1:
                    transpose_conv(i - 1)
            transpose_conv(CONVS - 1)
            transpose_weights(W_END, 2 * NX)

            def transpose_y(c, first):
                pe.wait_ge(y_ready, c + 1)
                if first:
                    pe.wait_ge(conv_read, CONVS)
                for g in range(GP):
                    last = to_columns(bank[7][:, g * PAIR:(g + 1) * PAIR], yt[:, g, :])
                last.then_inc(y_T, 1)

            def gate(c):
                pe.wait_ge(yh_ready, c + 1)
                for g in range(GP):
                    last = MM(bank[7][0:PAIR, g * E:(g + 1) * E], y32[:, g * PAIR:(g + 1) * PAIR], gwT[:, :], start=True, stop=True)
                last.then_inc(gate_done, 1)

            def transpose_cw(c):
                pe.wait_ge(cw_ready, c + 1)
                to_columns(bank[7][0:GP * E, 0:PAIR], cw[:, :, :].rearrange("p g e -> p (g e)")).then_inc(cw_T, 1)

            def three(dst, hi_w, lo_w, hi_x, lo_x, start, stop):
                MM(dst, hi_w, hi_x, start=start, stop=False)
                MM(dst, hi_w, lo_x, start=False, stop=False)
                return MM(dst, lo_w, hi_x, start=False, stop=stop)

            def up(c, e, first):
                tok = bass.ds(GT * c, GT)
                for o in range(FO):
                    if not (first and e == 0):
                        pe.wait_ge(act_done, FO * (NX * c + e - 1) + o + 1)
                    blk = slice(o * 128, (o + 1) * 128)
                    three(bank[o][:, 0:GT], w1h[:, e, blk], w1l[:, e, blk], yh[:, tok], yl[:, tok], True, True).then_inc(up_done, 1)

            def down(c, e, first):
                unit = max(e - 1, 0)
                if e != 1 and not (first and unit < 3):
                    pe.wait_ge(scaled, 9 * c + unit - 2)
                for o in range(FO):
                    if o % 2 == 0:
                        pe.wait_ge(split_done, 2 * (NX * c + e) + o // 2 + 1)
                    last = three(bank[4 + unit % 3][:, 0:GT], w2h[:, e, o, :], w2l[:, e, o, :], gh[e % 2][:, o, :], gl[e % 2][:, o, :],
                                 o == 0 and e != 1, o == FO - 1 and e != 0)
                last.then_inc(down_done, 1)

            def output(c, last):
                pe.wait_ge(added, E * (c + 1))
                if not last:
                    pe.wait_ge(cwT_ready, c + 2)
                for g in range(GP):
                    last = TP(bank[7][0:PAIR, g * D:(g + 1) * D], acc[:, g * PAIR:(g + 1) * PAIR], ident[:, :])
                last.then_inc(out_T, 1)

            def chunk(c, first, last):
                for e in range(NX):
                    if e + 1 < NX:
                        up(c, e + 1, first)
                    elif not last:
                        pe.wait_ge(yl_ready, c + 2)
                        up(c + 1, 0, False)
                    if e == 1 and not first:
                        output(c - 1, False)
                    if e == 3 and first:
                        transpose_cw(0)
                    if not last:
                        if e == 3 and not first:
                            pe.wait_ge(out_ready, c)
                            transpose_y(c + 1, False)
                        if e == 4:
                            gate(c + 1)
                        if e == 9:
                            transpose_cw(c + 1)
                    down(c, e, first)
                    if e == 3 and first:
                        pe.wait_ge(cwT_ready, 1)
                        transpose_y(1, False)

            transpose_y(0, True)
            gate(0)
            pe.wait_ge(w_lo, 2 * NX)
            pe.wait_ge(yl_ready, 1)
            up(0, 0, True)
            chunk(0, True, False)
            with pe.Fori(1, NG - 1) as c:
                chunk(c, False, False)
            chunk(NG - 1, False, True)
            pe.wait_ge(out_ready, NG - 1)
            output(NG - 1, True)


_INS = ["x", "L0_tok_W_patch", "L0_tok_b_patch", "L0_tok_pos_embed", "L0_tok_W_coord", "L0_tok_b_coord",
        "L0_tok_W_spinor", "L0_tok_b_spinor", "L0_tok_W_embed", "L0_tok_b_embed", "L0_tok_ln_gamma",
        "L0_tok_ln_beta", "L0_tok_W_out", "L0_tok_b_out", "L0_attn_Lambda_re", "L0_attn_Lambda_im",
        "L0_attn_P", "L0_attn_B", "L0_attn_C", "L0_attn_D", "L0_attn_log_step", "L0_ffn_gate_w",
        "L0_ffn_gate_b", "L0_ffn_sw1", "L0_ffn_sb1", "L0_ffn_sw2", "L0_ffn_sb2", "L0_ffn_rw1",
        "L0_ffn_rb1", "L0_ffn_rw2", "L0_ffn_rb2"]


def kernel(**inputs):
    import numpy as _np
    import concourse.bacc as _bacc
    from concourse import mybir as _mybir
    from concourse.bass_utils import run_bass_kernel_spmd as _run

    nc = _bacc.Bacc("TRN2", target_bir_lowering=False, num_devices=1)
    arrays, args = {}, []
    n = _np.arange(L)
    tan = _np.tan(_np.pi * n / L)
    angle = 2 * _np.pi * (n[:, None] * n[None, ::-1] % L) / L
    tables = {
        "ident": _np.eye(128, dtype=_np.float32),
        "tan": _np.stack([2 * tan, tan]).astype(_np.float32),
        "dft": (_np.concatenate([_np.cos(angle), -_np.sin(angle)], 1) / L).astype(_np.float32),
    }
    for name in _INS:
        arrays[f"in_{name}"] = _np.ascontiguousarray(inputs[name])
    for name, a in tables.items():
        arrays[f"table_{name}"] = a
    for name, a in arrays.items():
        args.append(nc.dram_tensor(name, a.shape, _mybir.dt.from_np(a.dtype), kind="ExternalInput").ap())
    args.append(nc.dram_tensor("out", (B, L, D), _mybir.dt.float32, kind="ExternalOutput").ap())
    tower(nc, *args)
    r = _run(nc, [arrays], core_ids=[0])
    return r.results[0]["out"]
```
